# Optimizing a Trainium2 kernel written in Bass

```python
import numpy as np
import jax
import jax.numpy as jnp

def _softmax(x, axis=-1):
    return jax.nn.softmax(x, axis=axis)

def _gelu(x):
    return jax.nn.gelu(x, approximate=True)

def _silu(x):
    return jax.nn.silu(x)

def _sigmoid(x):
    return jax.nn.sigmoid(x)

def _layernorm(x, axis=-1, eps=1e-05):
    m = jnp.mean(x, axis=axis, keepdims=True)
    v = jnp.var(x, axis=axis, keepdims=True)
    return (x - m) / jnp.sqrt(v + eps)

def _scatter_add(tgt, idx, src, axis=0):
    return tgt.at[idx].add(src)

def _segment_sum(src, seg, n):
    return jax.ops.segment_sum(src, seg, n)
kernel_name = 'mk_cond_seq_d1_seqx_r2_bbc130'

def setup_inputs(seed: int=0):
    np.random.seed(seed)
    _w = jnp.asarray

    def _rec_inputs():
        import jax
        import jax.numpy as jnp
        _rk = jax.random.key(seed)
        x = -0.0002928 + 1 * jax.random.normal(jax.random.fold_in(_rk, 1), (2, 2048, 512), jnp.float32)
        _lenS = 2048 - jax.random.randint(jax.random.fold_in(_rk, 7), (2,), 0, max(1, 2048 // 4) + 1, jnp.int32)
        _lenS2 = 2048 - jax.random.randint(jax.random.fold_in(_rk, 8), (2,), 0, max(1, 2048 // 4) + 1, jnp.int32)
        cond_1024 = 0.000887014 + 1.03683 * jax.random.normal(jax.random.fold_in(_rk, 11), (2, 512), jnp.float32)
        return (x, cond_1024)
    x, cond_1024 = _rec_inputs()

    def _L0_cond_setup():
        import jax, jax.numpy as jnp
        import numpy as np
        D = 512
        H = 16
        DH = D // H
        FF = int(D * 2.0)
        EPS = 1e-06

        def _ln(t):
            mu = jnp.mean(t, axis=-1, keepdims=True)
            var = jnp.mean((t - mu) ** 2, axis=-1, keepdims=True)
            return (t - mu) * jax.lax.rsqrt(var + EPS)
        key = jax.random.key(seed)
        ks = jax.random.split(key, 16)
        B, L = (2, 1024)
        s = 0.02
        return {'x': jax.random.normal(ks[0], (B, L, D), jnp.float32), 'c': jax.random.normal(ks[1], (B, 1, D), jnp.float32), 'Wq': jax.random.normal(ks[2], (D, D), jnp.float32) * s, 'bq': jnp.zeros((D,), jnp.float32), 'Wk': jax.random.normal(ks[3], (D, D), jnp.float32) * s, 'bk': jnp.zeros((D,), jnp.float32), 'Wv': jax.random.normal(ks[4], (D, D), jnp.float32) * s, 'bv': jnp.zeros((D,), jnp.float32), 'Wo': jax.random.normal(ks[5], (D, D), jnp.float32) * s, 'bo': jnp.zeros((D,), jnp.float32), 'W1': jax.random.normal(ks[6], (D, FF), jnp.float32) * s, 'b1': jnp.zeros((FF,), jnp.float32), 'W2': jax.random.normal(ks[7], (FF, D), jnp.float32) * s, 'b2': jnp.zeros((D,), jnp.float32), 'Wada': jax.random.normal(ks[8], (D, 6 * D), jnp.float32) * s, 'bada': jnp.zeros((6 * D,), jnp.float32)}
    _L0_cond_all = _L0_cond_setup()
    _L0_cond_in = {k: v for k, v in _L0_cond_all.items() if k in ('Wq', 'bq', 'Wk', 'bk', 'Wv', 'bv', 'Wo', 'bo', 'W1', 'b1', 'W2', 'b2', 'Wada', 'bada')}
    del _L0_cond_all
    return {'x': x, 'cond_1024': cond_1024, 'L0_cond_Wq': _L0_cond_in['Wq'], 'L0_cond_bq': _L0_cond_in['bq'], 'L0_cond_Wk': _L0_cond_in['Wk'], 'L0_cond_bk': _L0_cond_in['bk'], 'L0_cond_Wv': _L0_cond_in['Wv'], 'L0_cond_bv': _L0_cond_in['bv'], 'L0_cond_Wo': _L0_cond_in['Wo'], 'L0_cond_bo': _L0_cond_in['bo'], 'L0_cond_W1': _L0_cond_in['W1'], 'L0_cond_b1': _L0_cond_in['b1'], 'L0_cond_W2': _L0_cond_in['W2'], 'L0_cond_b2': _L0_cond_in['b2'], 'L0_cond_Wada': _L0_cond_in['Wada'], 'L0_cond_bada': _L0_cond_in['bada']}

def reference(x, cond_1024, L0_cond_Wq, L0_cond_bq, L0_cond_Wk, L0_cond_bk, L0_cond_Wv, L0_cond_bv, L0_cond_Wo, L0_cond_bo, L0_cond_W1, L0_cond_b1, L0_cond_W2, L0_cond_b2, L0_cond_Wada, L0_cond_bada):
    import jax
    import jax.numpy as jnp

    def _L0_cond_ref(x, c, Wq, bq, Wk, bk, Wv, bv, Wo, bo, W1, b1, W2, b2, Wada, bada):
        import jax, jax.numpy as jnp
        import numpy as np
        D = 512
        H = 16
        DH = D // H
        FF = int(D * 2.0)
        EPS = 1e-06

        def _ln(t):
            mu = jnp.mean(t, axis=-1, keepdims=True)
            var = jnp.mean((t - mu) ** 2, axis=-1, keepdims=True)
            return (t - mu) * jax.lax.rsqrt(var + EPS)
        B, L, _ = x.shape
        ada = jax.nn.silu(c) @ Wada + bada
        shift_msa, scale_msa, gate_msa, shift_mlp, scale_mlp, gate_mlp = jnp.split(ada, 6, axis=-1)
        h = _ln(x) * (1.0 + scale_msa) + shift_msa
        q = (h @ Wq + bq).reshape(B, L, H, DH)
        k = (h @ Wk + bk).reshape(B, L, H, DH)
        v = (h @ Wv + bv).reshape(B, L, H, DH)
        scale = 1.0 / np.sqrt(DH).astype(np.float32)
        scores = jnp.einsum('blhe,bshe->bhls', q, k)
        A = jax.nn.softmax(scale * scores, axis=-1)
        out = jnp.einsum('bhls,bshd->blhd', A, v)
        out = jnp.transpose(out, (0, 2, 1, 3)).reshape(B, L, H * DH)
        x = x + gate_msa * (out @ Wo + bo)
        h2 = _ln(x) * (1.0 + scale_mlp) + shift_mlp
        m = jax.nn.gelu(h2 @ W1 + b1, approximate=False) @ W2 + b2
        return x + gate_mlp * m
    x = _L0_cond_ref(x, cond_1024[:, None, :], L0_cond_Wq, L0_cond_bq, L0_cond_Wk, L0_cond_bk, L0_cond_Wv, L0_cond_bv, L0_cond_Wo, L0_cond_bo, L0_cond_W1, L0_cond_b1, L0_cond_W2, L0_cond_b2, L0_cond_Wada, L0_cond_bada)
    return x

_drawn_inputs = setup_inputs


def setup_inputs(seed=0):
    import zlib

    import numpy as np

    out = dict(_drawn_inputs(seed))
    spreads = {'L0_cond_bq': (0.0, 0.8),
     'L0_cond_bk': (0.0, 0.8),
     'L0_cond_bv': (0.0, 0.666),
     'L0_cond_bo': (0.0, 0.272),
     'L0_cond_b1': (0.0, 0.72),
     'L0_cond_b2': (0.0, 0.296),
     'L0_cond_bada': (0.0, 0.318)}
    factors = {'L0_cond_Wq': 8.0, 'L0_cond_Wk': 8.0, 'L0_cond_Wv': 3.212}
    for name, (base, spread) in spreads.items():
        noise = np.random.default_rng([zlib.crc32(name.encode()), seed]).standard_normal(out[name].shape)
        drawn = base * np.exp(spread * noise) if base else spread * noise
        out[name] = jnp.asarray(drawn.astype(out[name].dtype))
    for name, factor in factors.items():
        out[name] = (out[name] * factor).astype(out[name].dtype)
    return out
```

```python
from contextlib import ExitStack

import concourse.bass as bass
from concourse import mybir

F32 = mybir.dt.float32
F32R = mybir.dt.float32r
ALU = mybir.AluOpType
ACT = mybir.ActivationFunctionType
AX = mybir.AxisListType

P = 128
B, L, D, H = 2, 2048, 512, 16
DH = D // H
FF = 2 * D
EPS = 1e-6
SCALE = float(DH) ** -0.5
KC = D // P
FB = FF // P
CH = 512
TT = CH // P
CPB = L // CH
NCHUNK = B * CPB
G = B * H
NT = L // P
NQ = L // CH
MIX = D // DH
RING = 4
NBUF = 3
M_ROW = 3 * DH
POOL_TILES = [0, 1, 3, 4, 6, 7, 9, 10, 12]
PE_TILES = [t for t in range(NT) if t not in POOL_TILES]
NADD = len(POOL_TILES) - 1
START = 1
LOADS = 7


def block_kernel(nc, x, cT, wq, wk, wv, wo, w1, w2, wada, bqT, bkT, b1T, badaT, bada, bv, bo, b2, out):
    qk_hi = [nc.dram_tensor(f"{n}_hi", [B * D, L], F32, kind="Internal").ap() for n in "qk"]
    qk_lo = [nc.dram_tensor(f"{n}_lo", [B * D, L], F32, kind="Internal").ap() for n in "qk"]
    v_dram = nc.dram_tensor("v_rows", [L, B * D], F32, kind="Internal").ap()
    att_dram = nc.dram_tensor("attention_T", [D, B * L], F32, kind="Internal").ap()

    with ExitStack() as ctx:
        def sb(name, shape, dt=F32):
            return ctx.enter_context(nc.sbuf_tensor(name, shape, dt))

        def sem(name):
            return ctx.enter_context(nc.semaphore(name))

        weights_r = sb("weights_r", [P, 12288], F32R)
        w2_r = sb("w2_r", [P, 2, FB, D], F32R)
        acts_r = sb("acts_r", [P, 12288], F32R)
        work = sb("work", [P, 13312])
        ps = ctx.enter_context(nc.psum_tensor("ps", [P, 8, 512], F32))

        def view(t, at, *shape):
            n = 1
            for s in shape:
                n *= s
            ap = t[:, at:at + n]
            names = "abcd"[:len(shape)]
            if len(shape) == 1:
                return ap
            return ap.rearrange(f"p ({' '.join(names)}) -> p {' '.join(names)}",
                                **{k: s for k, s in zip(names[1:], shape[1:])})

        wqkv = view(weights_r, 0, 2, KC, 3 * D)
        wo_r = view(weights_r, 0, 2, KC, D)
        w1_r = view(weights_r, 2 * KC * D, 2, KC, FF)
        hT = [view(acts_r, b * 2 * KC * CH, 2, KC, CH) for b in range(2)]
        qs = [view(acts_r, 4096 * u, L) for u in range(NBUF)]
        ks = [view(acts_r, 4096 * u + L, L) for u in range(NBUF)]
        oT_r = view(acts_r, 0, 2, KC, CH)
        h2T = view(acts_r, 2 * KC * CH, 2, KC, CH)
        g_r = view(acts_r, 4 * KC * CH, 4, 2, CH)

        x1c = [view(work, 2048 * b, TT, D) for b in range(2)]
        hTf1 = view(work, 4096, KC, CH)
        qk_st = view(work, 6144, 2, 2, CH)
        v_st = view(work, 8192, 2, D)
        stage = [view(work, 9216 + 2048 * s, KC, D) for s in range(2)]
        v_sb = [view(work, 512 * u, NT, DH) for u in range(NBUF)]
        psum_acc = view(work, 1536, L)
        o_st = [view(work, 3584 + 512 * u, CH) for u in range(NBUF)]
        prob = view(work, 5120, RING, L)
        xc = [view(work, 2048 * b, TT, D) for b in range(2)]
        xn3 = view(work, 4096, TT, D)
        oTf = [view(work, 6144 + 2048 * b, KC, CH) for b in range(2)]
        hTf3 = view(work, 10240, KC, CH)
        gf = view(work, 12288, 2, CH)

        tmp3 = sb("tmp3", [P, 2, D])
        gate = sb("gate", [P, 2, B, D])
        gate_b = sb("gate_b", [P, 2, B, D])
        bv_rows = sb("bv_rows", [P, D])
        mod = sb("mod", [P, 4, KC, B])
        ident = sb("ident", [P, P])
        ones = sb("ones", [P, P])
        recip = sb("recip", [P, CH])
        c_sb = sb("c_sb", [P, KC, B])
        cs = sb("cs", [P, KC, B])
        bq_sb = sb("bq_sb", [P, 2, KC])
        b1_sb = sb("b1_sb", [P, FB])
        bada_sb = sb("bada_sb", [P, 6, KC])
        stats = sb("stats", [P, TT, 6])
        mv = sb("mv", [P, TT, 2])
        var_eps = sb("var_eps", [P, TT])
        minus_half = sb("minus_half", [P, TT])
        rstd = sb("rstd", [P, TT])
        part_max = sb("part_max", [P, NT, 2])
        row_max = sb("row_max", [P, NT])
        neg_max = sb("neg_max", [NT, P], F32R)
        cs_wide = view(work, 4096, KC, B, P)
        bias_wide = view(work, 6144, 2, D)
        bias_rows = view(work, 7168, 3, D)[0:1]
        gate_rows = view(work, 5120, 2, D)[0:1]

        consts_in = sem("consts_in")
        staged = [sem(f"staged{s}") for s in range(2)]
        ident_ok = sem("ident_ok")
        ones_ok = sem("ones_ok")
        silu_ok = sem("silu_ok")
        wide_ok = sem("wide_ok")
        ada_mm = sem("ada_mm")
        mod_ok = sem("mod_ok")
        bias_mm = sem("bias_mm")
        bias_ok = sem("bias_ok")
        gateb_ok = sem("gateb_ok")
        w_hi = sem("w_hi")
        w_lo = sem("w_lo")

        x_in = [sem(f"x_in{b}") for b in range(2)]
        stats_ok = sem("stats_ok")
        mv_ok = sem("mv_ok")
        eps_ok = sem("eps_ok")
        rstd_ok = sem("rstd_ok")
        xn_ok = sem("xn_ok")
        xT_mm = sem("xT_mm")
        hT_hi = sem("hT_hi")
        hT_lo = sem("hT_lo")
        qkv_mm = sem("qkv_mm")
        qk_hi_ok = sem("qk_hi_ok")
        qk_lo_ok = sem("qk_lo_ok")
        v_ok = sem("v_ok")
        qk_out = [sem(f"qk_out{s}") for s in range(2)]
        v_out = [sem(f"v_out{s}") for s in range(2)]

        ones_row = sem("ones_row")
        head_in = [sem(f"head_in{u}") for u in range(NBUF)]
        a_mm = sem("a_mm")
        a_max = sem("a_max")
        max_ok = sem("max_ok")
        maxT_mm = sem("maxT_mm")
        neg_ok = sem("neg_ok")
        neg_in = sem("neg_in")
        b_mm = sem("b_mm")
        exp_ok = sem("exp_ok")
        pv_mm = sem("pv_mm")
        add_ok = sem("add_ok")
        den_mm = sem("den_mm")
        rec_ok = sem("rec_ok")
        o_ok = sem("o_ok")
        o_out = [sem(f"o_out{u}") for u in range(NBUF)]

        xc_in = [sem(f"xc_in{b}") for b in range(2)]
        oT_in = [sem(f"oT_in{b}") for b in range(2)]
        oT_hi = sem("oT_hi")
        oT_lo = sem("oT_lo")
        o_mm = sem("o_mm")
        xg_ok = sem("xg_ok")
        o_tmp = sem("o_tmp")
        x1_ok = sem("x1_ok")
        stats3 = sem("stats3")
        mv3 = sem("mv3")
        eps3 = sem("eps3")
        rstd3 = sem("rstd3")
        xn3_ok = sem("xn3_ok")
        h2_mm = sem("h2_mm")
        h2_hi = sem("h2_hi")
        h2_lo = sem("h2_lo")
        m1_mm = sem("m1_mm")
        gelu_ok = sem("gelu_ok")
        g_hi = sem("g_hi")
        g_lo = sem("g_lo")
        m2_used = sem("m2_used")
        x1g_ok = sem("x1g_ok")
        m2_tmp = sem("m2_tmp")
        y_ok = sem("y_ok")
        y_out = [sem(f"y_out{b}") for b in range(2)]

        start_at_one = [pv_mm, add_ok, m1_mm, hT_lo, h2_lo, g_lo, m2_used, y_ok, hT_hi, h2_hi, v_ok, exp_ok, o_ok, gelu_ok, den_mm,
                        *v_out, *o_out]

        block = ctx.enter_context(nc.Block())

        def rows_of(w, c0):
            return w[:, c0:c0 + D].rearrange("(k p) n -> p k n", p=P)

        early = [("ada", n, rows_of(wada, n * D)) for n in (0, 1)]
        early += [("w", n, rows_of(w, 0)) for n, w in enumerate((wq, wk, wv))]
        early += [("ada", n, rows_of(wada, n * D)) for n in (2, 3, 4, 5)]
        early += [("w", 3 + n, w2[n * D:(n + 1) * D, :].rearrange("(k p) n -> p k n", p=P)) for n in range(2)]
        late = [("w", 5, rows_of(wo, 0)), ("w", 6, rows_of(w1, 0)), ("w", 7, rows_of(w1, D))]
        pieces = early + late
        ADA_ORDER = [n for kind, n, _ in pieces if kind == "ada"]
        N_CONST = 10

        def split_of(n):
            if n < 3:
                return [wqkv[:, s, :, n * D:(n + 1) * D] for s in range(2)]
            if n < 5:
                return [w2_r[:, s, (n - 3) * KC:(n - 2) * KC, :] for s in range(2)]
            if n == 5:
                return [wo_r[:, s] for s in range(2)]
            return [w1_r[:, s, :, (n - 6) * D:(n - 5) * D] for s in range(2)]

        MM_CHUNK = 2 * KC + TT
        MOD_SHIFT1, MOD_SCALE1, MOD_SHIFT2, MOD_SCALE2 = range(4)
        MOD_OF = {0: MOD_SHIFT1, 1: MOD_SCALE1, 3: MOD_SHIFT2, 4: MOD_SCALE2}
        GATE_OF = {2: 0, 5: 1}

        @block.sync
        def _(sp):
            for s in start_at_one:
                sp.sem_inc(s, START)

            def load_x(b, c, dst, s):
                sp.dma_start(dst[b], x[b, bass.ds(c * CH, CH), :].rearrange("(t p) d -> p t d", p=P)).then_inc(s[b], 16)

            def load_x_mixed(b, c):
                sp.dma_start(x1c[b], x[b].rearrange("(p r) d -> p r d", r=MIX)[:, bass.ds(c * TT, TT), :]).then_inc(x_in[b], 16)

            def load_piece(k):
                if k >= 2:
                    kind, n, _ = pieces[k - 2]
                    if kind == "ada":
                        sp.wait_ge(ada_mm, ADA_ORDER.index(n) + 1)
                    else:
                        sp.wait_ge(w_hi, n + 1)
                        sp.wait_ge(w_lo, n + 1)
                sp.dma_start(stage[k % 2], pieces[k][2]).then_inc(staged[k % 2], 16)

            sp.dma_start(c_sb[:], cT).then_inc(consts_in, 16)
            load_piece(0)
            load_piece(1)
            load_x_mixed(0, 0)
            load_x_mixed(1, 0)
            sp.dma_start(bq_sb[:, 0, :], bqT).then_inc(consts_in, 16)
            sp.dma_start(bq_sb[:, 1, :], bkT).then_inc(consts_in, 16)
            sp.dma_start(b1_sb[:], b1T).then_inc(consts_in, 16)
            sp.dma_start(bada_sb[:], badaT).then_inc(consts_in, 16)
            for n, r in enumerate((bv, bo, b2)):
                sp.dma_start(bias_rows[:, n, :], r.rearrange("(o d) -> o d", o=1)).then_inc(consts_in, 16)
            for n, r in enumerate((bada[2 * D:3 * D], bada[5 * D:6 * D])):
                sp.dma_start(gate_rows[:, n, :], r.rearrange("(o d) -> o d", o=1)).then_inc(consts_in, 16)
            for k in range(2, len(early)):
                load_piece(k)

            def store_qkv(c, b, n):
                for m in range(2 * KC):
                    t, blk = m // KC, m % KC
                    at = slice(b * D + blk * P, b * D + (blk + 1) * P)
                    sp.wait_ge(qk_lo_ok, n * 2 * KC + m + 1)
                    sp.dma_start(qk_hi[t][at, bass.ds(c * CH, CH)], qk_st[:, m % 2, 0, :]).then_inc(qk_out[m % 2], 16)
                    sp.dma_start(qk_lo[t][at, bass.ds(c * CH, CH)], qk_st[:, m % 2, 1, :]).then_inc(qk_out[m % 2], 16)
                for t in range(TT):
                    sp.wait_ge(v_ok, START + n * TT + t + 1)
                    sp.dma_start(v_dram[bass.ds(c * CH + t * P, P), b * D:(b + 1) * D], v_st[:, t % 2, :]).then_inc(v_out[t % 2], 16)

            def stage1(c, b, more):
                n = c * 2 + b
                if more:
                    sp.wait_ge(xT_mm, n * KC + KC)
                    load_x_mixed(b, c + 1)
                store_qkv(c, b, n)

            with sp.Fori(0, CPB - 1) as c:
                for b in range(2):
                    stage1(c, b, True)
            for b in range(2):
                stage1(CPB - 1, b, False)

            for k in range(len(early), len(pieces)):
                load_piece(k)

            for s in range(2):
                sp.wait_ge(qk_out[s], 16 * 2 * NCHUNK * KC)
                sp.wait_ge(v_out[s], START + 16 * NCHUNK * TT // 2)

            def load_head(g, u):
                r = bass.ds(g * DH, DH)
                for blk, (q, k) in enumerate(((qk_hi, qk_hi), (qk_hi, qk_lo), (qk_lo, qk_hi))):
                    at = slice(blk * DH, (blk + 1) * DH)
                    sp.dma_start(qs[u][at, :].bitcast(F32), q[0][r, :]).then_inc(head_in[u], 16)
                    sp.dma_start(ks[u][at, :].bitcast(F32), k[1][r, :]).then_inc(head_in[u], 16)
                sp.dma_start(v_sb[u], v_dram[:, r].rearrange("(t p) d -> p t d", p=P)).then_inc(head_in[u], 16)

            def put_max(g, u):
                sp.wait_ge(neg_ok, g + 1)
                sp.dma_start(qs[u][M_ROW:M_ROW + 1, :].bitcast(F32),
                             neg_max[:].bitcast(F32)).then_inc(neg_in, 16)

            def stage2(g, u, load, nxt):
                if load:
                    sp.wait_ge(den_mm, START + g)
                    load_head(g + 2, (u + 2) % NBUF)
                if nxt:
                    put_max(g + 1, (u + 1) % NBUF)
                sp.wait_ge(o_ok, START + g + 1)
                for j in range(NQ):
                    sp.dma_start(att_dram[j * P:(j + 1) * P, bass.ds(g * P, P)].rearrange("(r d) q -> d r q", d=DH),
                                 o_st[u][j * DH:(j + 1) * DH, :].rearrange("d (r q) -> d r q", q=P)).then_inc(o_out[u], 16)

            load_head(0, 0)
            load_head(1, 1)
            put_max(0, 0)
            with sp.Fori(0, G // NBUF) as i:
                for u in range(NBUF):
                    stage2(i * NBUF + u, u, True, True)
            for g in range(G // NBUF * NBUF, G):
                stage2(g, g % NBUF, False, g + 1 < G)
            for u in range(NBUF):
                sp.wait_ge(o_out[u], START + 16 * NQ * len(range(u, G, NBUF)))

            def load_oT(b, c):
                sp.dma_start(oTf[b], att_dram[:, bass.ds(b * L + c * CH, CH)].rearrange("(k p) q -> p k q", p=P)).then_inc(oT_in[b], 16)

            for b in range(2):
                load_x(b, 0, xc, xc_in)
                load_oT(b, 0)

            def stage3(c, b, more):
                n = c * 2 + b
                if more:
                    sp.wait_ge(oT_lo, (n + 1) * KC)
                    sp.wait_ge(oT_hi, (n + 1) * KC)
                    load_oT(b, c + 1)
                sp.wait_ge(y_ok, START + (n + 1) * TT)
                sp.dma_start(out[b, bass.ds(c * CH, CH), :].rearrange("(t p) d -> p t d", p=P), xc[b]).then_inc(y_out[b], 16)
                if more:
                    sp.wait_ge(y_out[b], c * 16 + 16)
                    load_x(b, c + 1, xc, xc_in)

            with sp.Fori(0, CPB - 1) as c:
                for b in range(2):
                    stage3(c, b, True)
            for b in range(2):
                stage3(CPB - 1, b, False)
            for b in range(2):
                sp.wait_ge(y_out[b], 16 * CPB)

        @block.gpsimd
        def _(pool):
            nc.gpsimd.memset(ident[:], 0.0).then_inc(ident_ok, 1)
            pool.wait_ge(ident_ok, 1)
            nc.gpsimd.affine_select(out=ident[:], in_=ident[:], compare_op=ALU.not_equal, fill=1.0, base=0,
                                    pattern=[[-1, P]], channel_multiplier=1).then_inc(ident_ok, 1)
            nc.gpsimd.memset(minus_half[:], -0.5).then_inc(ident_ok, 1)
            pool.wait_ge(ident_ok, 3)

            def root(n, wait, added, done):
                pool.wait_ge(wait, (n + 1) * TT)
                nc.gpsimd.tensor_tensor(var_eps[:], var_eps[:], mv[:, :, 1], ALU.add).then_inc(added, 1)
                pool.wait_ge(added, n + 1)
                nc.gpsimd.tensor_tensor(rstd[:], var_eps[:], minus_half[:], ALU.pow).then_inc(done, 1)

            with pool.Fori(0, NCHUNK) as n:
                root(n, mv_ok, eps_ok, rstd_ok)

            def sum_probs(g):
                pool.wait_ge(den_mm, START + g)
                for k in range(NADD):
                    t = POOL_TILES[k + 1]
                    pool.wait_ge(exp_ok, START + g * (NT * NQ) + (t + 1) * NQ)
                    if k:
                        pool.wait_ge(add_ok, START + g * NADD + k)
                    first = prob[:, POOL_TILES[0] % RING, :] if k == 0 else psum_acc
                    nc.gpsimd.tensor_tensor(psum_acc, first, prob[:, t % RING, :], ALU.add).then_inc(add_ok, 1)

            with pool.Fori(0, G) as g:
                sum_probs(g)

            def add_bias(n, b, which, waits, done):
                for s, v in waits:
                    pool.wait_ge(s, v)
                for t in range(TT):
                    nc.gpsimd.tensor_tensor(xc[b][:, t, :], xc[b][:, t, :], gate_b[:, which, b, :], ALU.add).then_inc(done, 1)

            add_bias(0, 0, 0, [(xc_in[0], 16), (gateb_ok, 4)], xg_ok)
            root(0, mv3, eps3, rstd3)

            def stage3(c, b, nxt):
                n = c * 2 + b
                if nxt:
                    add_bias(n + 1, 1 - b, 0, [(xc_in[1 - b], (c + b) * 16 + 16)], xg_ok)
                add_bias(n, b, 1, [(xn3_ok, (n + 1) * TT)], x1g_ok)
                if nxt:
                    root(n + 1, mv3, eps3, rstd3)

            with pool.Fori(0, CPB - 1) as c:
                for b in range(2):
                    stage3(c, b, True)
            stage3(CPB - 1, 0, True)
            stage3(CPB - 1, 1, False)

        @block.scalar
        def _(act):
            act.wait_ge(consts_in, 16 * N_CONST)
            nc.scalar.activation(cs[:], c_sb[:], ACT.Silu).then_inc(silu_ok, 1)

            def split_hi(k):
                kind, n, _ = pieces[k]
                if kind == "w":
                    act.wait_ge(staged[k % 2], 16 * (k // 2 + 1))
                    nc.scalar.activation(split_of(n)[0], stage[k % 2], ACT.Copy).then_inc(w_hi, 1)

            for k in range(len(early)):
                split_hi(k)

            def modulate(n, b, xT, wait, used, hTf, h, shift, scale, done):
                for blk in range(KC):
                    act.wait_ge(wait, n * KC + blk + 1)
                    if used is not None:
                        act.wait_ge(used, START + n * KC)
                    kw = dict(scale=mod[:, scale, blk, b:b + 1], bias=mod[:, shift, blk, b:b + 1])
                    nc.scalar.activation(h[:, 0, blk, :], ps[:, xT + blk % 2, :], ACT.Identity, **kw)
                    nc.scalar.activation(hTf[:, blk, :], ps[:, xT + blk % 2, :], ACT.Identity, **kw).then_inc(done, 1)

            def hT1(c, b):
                n = c * 2 + b
                if not (isinstance(n, int) and n < 2):
                    act.wait_ge(qkv_mm, (n - 1) * MM_CHUNK)
                modulate(n, b, 0, xT_mm, hT_lo, hTf1, hT[b], MOD_SHIFT1, MOD_SCALE1, hT_hi)

            def heads_of_qk(c, b):
                n = c * 2 + b
                for m in range(2 * KC):
                    act.wait_ge(qkv_mm, n * MM_CHUNK + m + 1)
                    if not (isinstance(n, int) and n == 0 and m < 2):
                        act.wait_ge(qk_out[m % 2], (n * KC + m // 2) * 32)
                    nc.scalar.activation(qk_st[:, m % 2, 0, :].bitcast(F32R), ps[:, 2 + m % 4, :], ACT.Identity,
                                         bias=bq_sb[:, m // KC, m % KC:m % KC + 1]).then_inc(qk_hi_ok, 1)

            act.wait_ge(mod_ok, 6)
            act.wait_ge(gateb_ok, 4)
            hT1(0, 0)
            hT1(0, 1)
            heads_of_qk(0, 0)
            with act.Fori(1, CPB) as c:
                hT1(c, 0)
                heads_of_qk(c - 1, 1)
                hT1(c, 1)
                heads_of_qk(c, 0)
            heads_of_qk(CPB - 1, 1)

            act.wait_ge(qkv_mm, NCHUNK * MM_CHUNK)
            for k in range(len(early), len(pieces)):
                split_hi(k)
            act.wait_ge(w_lo, 8)

            def probs(g):
                for t in range(NT):
                    if t < RING:
                        act.wait_ge(pv_mm, START + g * NT)
                        if t == 0:
                            act.wait_ge(add_ok, START + g * NADD)
                    else:
                        act.wait_ge(pv_mm, START + g * NT + t - RING + 1)
                        if t - RING in POOL_TILES:
                            k = max(POOL_TILES.index(t - RING), 1)
                            act.wait_ge(add_ok, START + g * NADD + k)
                    for j in range(NQ):
                        act.wait_ge(b_mm, g * (NT * NQ) + t * NQ + j + 1)
                        nc.scalar.activation(prob[:, t % RING, j * CH:(j + 1) * CH], ps[:, 4 + j % 2, :],
                                             ACT.Exp, scale=SCALE).then_inc(exp_ok, 1)

            with act.Fori(0, G) as g:
                probs(g)

            def split_oT(n, b, c):
                act.wait_ge(oT_in[b], c * 16 + 16)
                if not isinstance(n, int) or n:
                    act.wait_ge(o_mm, n * TT)
                for blk in range(KC):
                    nc.scalar.activation(oT_r[:, 0, blk, :], oTf[b][:, blk, :], ACT.Copy).then_inc(oT_hi, 1)

            split_oT(0, 0, 0)

            def stage3(c, b, nxt):
                n = c * 2 + b
                if nxt:
                    split_oT(n + 1, 1 - b, c + b)
                act.wait_ge(m1_mm, START + n * FB)
                modulate(n, b, 0, h2_mm, h2_lo, hTf3, h2T, MOD_SHIFT2, MOD_SCALE2, h2_hi)
                for f in range(FB):
                    act.wait_ge(m1_mm, START + n * FB + f + 1)
                    if f >= 2:
                        act.wait_ge(g_lo, START + n * FB + f - 1)
                    else:
                        act.wait_ge(g_lo, START + n * FB)
                    nc.scalar.activation(gf[:, f % 2, :], ps[:, 2 + f % 2, :], ACT.Gelu, bias=b1_sb[:, f:f + 1]).then_inc(gelu_ok, 1)

            with act.Fori(0, CPB - 1) as c:
                for b in range(2):
                    stage3(c, b, True)
            stage3(CPB - 1, 0, True)
            stage3(CPB - 1, 1, False)

        @block.vector
        def _(dve):
            nc.vector.memset(ones[:], 1.0).then_inc(ones_ok, 1)
            dve.wait_ge(ones_ok, 1)
            dve.wait_ge(silu_ok, 1)
            for k in range(KC):
                for b in range(B):
                    nc.vector.tensor_scalar(cs_wide[:, k, b, :], ones[:], cs[:, k, b:b + 1], None, ALU.mult).then_inc(wide_ok, 1)

            def split_lo(k):
                kind, n, _ = pieces[k]
                if kind == "w":
                    dve.wait_ge(w_hi, n + 1)
                    hi, lo = split_of(n)
                    nc.vector.tensor_tensor(lo, stage[k % 2], hi.bitcast(F32), ALU.subtract).then_inc(w_lo, 1)

            def take_ada(n):
                at = ADA_ORDER.index(n)
                dve.wait_ge(ada_mm, at + 1)
                if n in MOD_OF:
                    for b in range(B):
                        ins = nc.vector.scalar_tensor_tensor(
                            out=mod[:, MOD_OF[n], :, b], in0=ps[:, 6, 0:KC * B].rearrange("p (k b) -> p k b", b=B)[:, :, b],
                            scalar=1.0 if n in (1, 4) else 0.0, in1=bada_sb[:, n, :], op0=ALU.add, op1=ALU.add)
                else:
                    for b in range(B):
                        ins = nc.vector.tensor_copy(gate[:, GATE_OF[n], b, :], ps[:, 6 + b, :])
                ins.then_inc(mod_ok, 1)

            for k in range(3):
                dve.wait_ge(bias_mm, k + 1)
                nc.vector.tensor_copy(bv_rows[:] if k == 0 else bias_wide[:, k - 1, :], ps[:, k, :]).then_inc(bias_ok, 1)
            for k, (kind, n, _) in enumerate(early):
                if kind == "ada":
                    take_ada(n)
                else:
                    split_lo(k)
            dve.wait_ge(bias_ok, 3)
            dve.wait_ge(mod_ok, 6)
            for w in range(2):
                for b in range(B):
                    nc.vector.tensor_tensor(gate_b[:, w, b, :], gate[:, w, b, :], bias_wide[:, w, :], ALU.mult).then_inc(gateb_ok, 1)

            def norm_stats(n, src, ok):
                for t in range(TT):
                    nc.vector.bn_stats(stats[:, t, :], src[:, t, :]).then_inc(ok, 1)

            def norm_mean(n, ok, done):
                dve.wait_ge(ok, (n + 1) * TT)
                nc.vector.memset(var_eps[:], EPS)
                for t in range(TT):
                    nc.vector.bn_aggr(mv[:, t, :], stats[:, t, :]).then_inc(done, 1)

            def norm_apply(n, src, dst, ok, done):
                dve.wait_ge(ok, n + 1)
                for t in range(TT):
                    nc.vector.tensor_scalar(dst[:, t, :], src[:, t, :], mv[:, t, 0:1], rstd[:, t:t + 1],
                                            ALU.subtract, ALU.mult).then_inc(done, 1)

            def norm1(c, b):
                n = c * 2 + b
                dve.wait_ge(x_in[b], c * 16 + 16)
                if not (isinstance(n, int) and n == 0):
                    dve.wait_ge(xn_ok, n * TT)
                norm_stats(n, x1c[b], stats_ok)
                norm_mean(n, stats_ok, mv_ok)
                norm_apply(n, x1c[b], x1c[b], rstd_ok, xn_ok)

            def remainders(n, hi_ok, hTf, h, done):
                for blk in range(KC):
                    dve.wait_ge(hi_ok, START + n * KC + blk + 1)
                    nc.vector.tensor_tensor(h[:, 1, blk, :], hTf[:, blk, :], h[:, 0, blk, :].bitcast(F32), ALU.subtract).then_inc(done, 1)

            def take_qkv(c, b):
                n = c * 2 + b
                for m in range(2 * KC):
                    dve.wait_ge(qk_hi_ok, n * 2 * KC + m + 1)
                    nc.vector.scalar_tensor_tensor(
                        out=qk_st[:, m % 2, 1, :].bitcast(F32R), in0=ps[:, 2 + m % 4, :], scalar=bq_sb[:, m // KC, m % KC:m % KC + 1],
                        in1=qk_st[:, m % 2, 0, :], op0=ALU.add, op1=ALU.subtract).then_inc(qk_lo_ok, 1)
                for t in range(TT):
                    dve.wait_ge(qkv_mm, n * MM_CHUNK + 2 * KC + t + 1)
                    dve.wait_ge(v_out[t % 2], START + (n * (TT // 2) + t // 2) * 16)
                    nc.vector.tensor_tensor(v_st[:, t % 2, :], ps[:, 2 + t % 4, :], bv_rows[:], ALU.add).then_inc(v_ok, 1)

            norm1(0, 0)
            norm1(0, 1)
            remainders(0, hT_hi, hTf1, hT[0], hT_lo)
            with dve.Fori(0, CPB - 1) as c:
                remainders(c * 2 + 1, hT_hi, hTf1, hT[1], hT_lo)
                norm1(c + 1, 0)
                take_qkv(c, 0)
                remainders(c * 2 + 2, hT_hi, hTf1, hT[0], hT_lo)
                norm1(c + 1, 1)
                take_qkv(c, 1)
            remainders(NCHUNK - 1, hT_hi, hTf1, hT[1], hT_lo)
            take_qkv(CPB - 1, 0)
            take_qkv(CPB - 1, 1)

            dve.wait_ge(qkv_mm, NCHUNK * MM_CHUNK)
            for u in range(NBUF):
                nc.vector.memset(ks[u][M_ROW:M_ROW + 1, :].bitcast(F32), 1.0).then_inc(ones_row, 1)
            for k in range(len(early), len(pieces)):
                split_lo(k)

            def find_max(g):
                for t in range(NT):
                    for s in range(2):
                        dve.wait_ge(a_mm, g * (2 * NT) + 2 * t + s + 1)
                        nc.vector.tensor_reduce(part_max[:, t, s:s + 1], ps[:, 2 * s:2 * s + 2, :], AX.XY, ALU.max).then_inc(a_max, 1)
                dve.wait_ge(a_max, (g + 1) * (2 * NT))
                nc.vector.tensor_reduce(row_max[:], part_max[:], AX.X, ALU.max).then_inc(max_ok, 1)
                dve.wait_ge(maxT_mm, g + 1)
                if not isinstance(g, int) or g:
                    dve.wait_ge(neg_in, g * 16)
                nc.vector.tensor_scalar(neg_max[:], ps[0:NT, 0, 0:P], -1.0, None, ALU.mult).then_inc(neg_ok, 1)

            def normalise(g, u, uses):
                dve.wait_ge(den_mm, START + g + 1)
                nc.vector.reciprocal(recip[:], ps[:, 7, :]).then_inc(rec_ok, 1)
                dve.wait_ge(rec_ok, g + 1)
                dve.wait_ge(o_out[u], START + uses * (16 * NQ))
                nc.vector.tensor_tensor(o_st[u], ps[:, 6, :], recip[:], ALU.mult).then_inc(o_ok, 1)

            find_max(0)
            with dve.Fori(0, G // NBUF) as i:
                for u in range(NBUF):
                    find_max(i * NBUF + u + 1)
                    normalise(i * NBUF + u, u, i)
            for g in range(G // NBUF * NBUF, G):
                if g + 1 < G:
                    find_max(g + 1)
                normalise(g, g % NBUF, g // NBUF)

            def oT_rest(n, b):
                for blk in range(KC):
                    dve.wait_ge(oT_hi, n * KC + blk + 1)
                    nc.vector.tensor_tensor(oT_r[:, 1, blk, :], oTf[b][:, blk, :], oT_r[:, 0, blk, :].bitcast(F32), ALU.subtract).then_inc(oT_lo, 1)

            def residual1(n, b):
                for t in range(TT):
                    dve.wait_ge(o_mm, n * TT + t + 1)
                    nc.vector.tensor_tensor(xn3[:, t, :], ps[:, t % 2, :], gate[:, 0, b, :], ALU.mult).then_inc(o_tmp, 1)
                    dve.wait_ge(xg_ok, n * TT + t + 1)
                    dve.wait_ge(o_tmp, n * TT + t + 1)
                    nc.vector.tensor_tensor(xc[b][:, t, :], xc[b][:, t, :], xn3[:, t, :], ALU.add).then_inc(x1_ok, 1)

            def stats_of(n, b):
                dve.wait_ge(x1_ok, (n + 1) * TT)
                norm_stats(n, xc[b], stats3)

            def split_gelu(n, f):
                dve.wait_ge(gelu_ok, START + n * FB + f + 1)
                if f >= 4:
                    dve.wait_ge(m2_used, START + n * FB + f - 3)
                else:
                    dve.wait_ge(m2_used, START + n * FB)
                nc.vector.tensor_copy(g_r[:, f % 4, 0, :], gf[:, f % 2, :]).then_inc(g_hi, 1)
                dve.wait_ge(g_hi, n * FB + f + 1)
                nc.vector.tensor_tensor(g_r[:, f % 4, 1, :], gf[:, f % 2, :], g_r[:, f % 4, 0, :].bitcast(F32), ALU.subtract).then_inc(g_lo, 1)

            def residual2(n, b):
                dve.wait_ge(m2_used, START + (n + 1) * FB)
                for t in range(TT):
                    if t >= 2:
                        dve.wait_ge(y_ok, START + n * TT + t - 1)
                    else:
                        dve.wait_ge(y_ok, START + n * TT)
                    nc.vector.tensor_tensor(tmp3[:, t % 2, :], ps[:, 4 + t, :], gate[:, 1, b, :], ALU.mult).then_inc(m2_tmp, 1)
                    dve.wait_ge(m2_tmp, n * TT + t + 1)
                    dve.wait_ge(x1g_ok, n * TT + t + 1)
                    nc.vector.tensor_tensor(xc[b][:, t, :], xc[b][:, t, :], tmp3[:, t % 2, :], ALU.add).then_inc(y_ok, 1)

            oT_rest(0, 0)
            residual1(0, 0)
            stats_of(0, 0)
            norm_mean(0, stats3, mv3)
            norm_apply(0, xc[0], xn3, rstd3, xn3_ok)

            def stage3(c, b, nxt):
                n = c * 2 + b
                if nxt:
                    oT_rest(n + 1, 1 - b)
                remainders(n, h2_hi, hTf3, h2T, h2_lo)
                if nxt:
                    residual1(n + 1, 1 - b)
                split_gelu(n, 0)
                if nxt:
                    stats_of(n + 1, 1 - b)
                split_gelu(n, 1)
                if nxt:
                    norm_mean(n + 1, stats3, mv3)
                split_gelu(n, 2)
                if nxt:
                    norm_apply(n + 1, xc[1 - b], xn3, rstd3, xn3_ok)
                for f in range(3, FB):
                    split_gelu(n, f)
                residual2(n, b)

            with dve.Fori(0, CPB - 1) as c:
                for b in range(2):
                    stage3(c, b, True)
            stage3(CPB - 1, 0, True)
            stage3(CPB - 1, 1, False)

        @block.tensor
        def _(pe):
            pe.wait_ge(ones_ok, 1)
            pe.wait_ge(consts_in, 16 * N_CONST)
            for k in range(3):
                nc.tensor.matmul(ps[:, k, :], ones[0:1, :], bias_rows[:, k, :], start=True, stop=True).then_inc(bias_mm, 1)

            def ada_piece(k, n):
                pe.wait_ge(staged[k % 2], 16 * (k // 2 + 1))
                at = ADA_ORDER.index(n)
                if at:
                    pe.wait_ge(mod_ok, at)
                w = stage[k % 2]
                if n in MOD_OF:
                    for blk in range(KC):
                        for kk in range(KC):
                            mm = nc.tensor.matmul(ps[:, 6, blk * B:(blk + 1) * B], w[:, kk, blk * P:(blk + 1) * P],
                                                  cs[:, kk, :], start=(kk == 0), stop=(kk == KC - 1))
                else:
                    for b in range(B):
                        for kk in range(KC):
                            nc.tensor.matmul(ps[:, 6 + b, :], cs_wide[:, kk, b, :], w[:, kk, :], start=(kk == 0), stop=False)
                        mm = nc.tensor.matmul(ps[:, 6 + b, :], ones[0:1, :], gate_rows[:, GATE_OF[n], :], start=False, stop=True)
                mm.then_inc(ada_mm, 1)

            pe.wait_ge(silu_ok, 1)
            pe.wait_ge(wide_ok, KC * B)
            for k, (kind, n, _) in enumerate(early):
                if kind == "ada":
                    ada_piece(k, n)

            def product(o, lhs, rhs):
                for kk in range(KC):
                    for s, r in ((0, 0), (0, 1), (1, 0)):
                        mm = nc.tensor.matmul(o, lhs(s, kk), rhs(r, kk), start=(kk == 0 and s == r), stop=(kk == KC - 1 and s == 1))
                return mm

            def transposes(n, src, wait, used, done):
                pe.wait_ge(wait, (n + 1) * TT)
                for blk in range(KC):
                    pe.wait_ge(used, START + n * KC + max(blk - 1, 0))
                    for t in range(TT):
                        mm = nc.tensor.transpose(ps[:, blk % 2, t * P:(t + 1) * P], src[:, t, blk * P:(blk + 1) * P], ident[:])
                    mm.then_inc(done, 1)

            def qkv(n, b):
                h = hT[b]
                pe.wait_ge(hT_lo, START + (n + 1) * KC)
                for m in range(2 * KC):
                    if m < 4:
                        pe.wait_ge(v_ok, START + n * TT)
                    else:
                        pe.wait_ge(qk_lo_ok, n * 2 * KC + m - 3)
                    product(ps[:, 2 + m % 4, :], lambda s, kk: wqkv[:, s, kk, m * P:(m + 1) * P],
                            lambda s, kk: h[:, s, kk, :]).then_inc(qkv_mm, 1)
                for t in range(TT):
                    pe.wait_ge(qk_lo_ok, n * 2 * KC + KC + t + 1)
                    product(ps[:, 2 + t % 4, :], lambda s, kk: h[:, s, kk, t * P:(t + 1) * P],
                            lambda s, kk: wqkv[:, s, kk, 2 * D:3 * D]).then_inc(qkv_mm, 1)

            pe.wait_ge(ident_ok, 3)
            pe.wait_ge(bias_ok, 3)
            transposes(0, x1c[0], xn_ok, hT_hi, xT_mm)
            pe.wait_ge(w_lo, 5)
            with pe.Fori(0, CPB - 1) as c:
                for b in range(2):
                    transposes(c * 2 + b + 1, x1c[1 - b], xn_ok, hT_hi, xT_mm)
                    qkv(c * 2 + b, b)
            transposes(NCHUNK - 1, x1c[1], xn_ok, hT_hi, xT_mm)
            qkv(NCHUNK - 2, 0)
            qkv(NCHUNK - 1, 1)

            def max_scores(g, u, t, s, first=False):
                if not (first and t == 0):
                    pe.wait_ge(a_max, g * (2 * NT) + 2 * t + s - 1)
                for j in range(2):
                    mm = nc.tensor.matmul(ps[:, 2 * s + j, :], qs[u][0:M_ROW, t * P:(t + 1) * P],
                                          ks[u][0:M_ROW, (2 * s + j) * CH:(2 * s + j + 1) * CH], start=True, stop=True)
                mm.then_inc(a_mm, 1)

            def transpose_max(g):
                pe.wait_ge(max_ok, g + 1)
                nc.tensor.matmul(ps[0:NT, 0, 0:P], row_max[:], ident[:], start=True, stop=True).then_inc(maxT_mm, 1)

            def scores(g, u, t, j):
                if t == 0 and j == 0:
                    pe.wait_ge(neg_in, g * 16 + 16)
                    pe.wait_ge(exp_ok, START + g * (NT * NQ))
                elif t or j > 1:
                    pe.wait_ge(exp_ok, START + g * (NT * NQ) + t * NQ + j - 1)
                nc.tensor.matmul(ps[:, 4 + j % 2, :], ks[u][0:M_ROW + 1, t * P:(t + 1) * P],
                                 qs[u][0:M_ROW + 1, j * CH:(j + 1) * CH], start=True, stop=True).then_inc(b_mm, 1)

            def denominators(src, first, last):
                for j in range(NQ):
                    mm = nc.tensor.matmul(ps[j * DH:(j + 1) * DH, 7, :], ones[:, 0:DH], src(j), start=first, stop=last)
                return mm

            def values(g, u, t):
                pe.wait_ge(exp_ok, START + g * (NT * NQ) + (t + 1) * NQ)
                if t == 0:
                    pe.wait_ge(o_ok, START + g)
                p = prob[:, t % RING, :]
                for j in range(NQ):
                    mm = nc.tensor.matmul(ps[j * DH:(j + 1) * DH, 6, :], v_sb[u][:, t, :], p[:, j * CH:(j + 1) * CH],
                                          start=(t == 0), stop=(t == NT - 1))
                if t in PE_TILES:
                    mm = denominators(lambda j: p[:, j * CH:(j + 1) * CH], t == PE_TILES[0], False)
                mm.then_inc(pv_mm, 1)

            def head(g, u, uses_next, nxt):
                un = (u + 1) % NBUF
                if nxt:
                    pe.wait_ge(head_in[un], uses_next * (16 * LOADS))
                    pe.wait_ge(neg_ok, g + 1)
                for t in range(NT):
                    if nxt:
                        max_scores(g + 1, un, t, 0)
                    scores(g, u, t, 0)
                    scores(g, u, t, 1)
                    if nxt:
                        max_scores(g + 1, un, t, 1)
                    scores(g, u, t, 2)
                    scores(g, u, t, 3)
                    if t:
                        values(g, u, t - 1)
                values(g, u, NT - 1)
                if nxt:
                    transpose_max(g + 1)
                pe.wait_ge(add_ok, START + (g + 1) * NADD)
                denominators(lambda j: psum_acc[:, j * CH:(j + 1) * CH], False, True).then_inc(den_mm, 1)

            pe.wait_ge(ones_row, NBUF)
            pe.wait_ge(v_ok, START + NCHUNK * TT)
            pe.wait_ge(head_in[0], 16 * LOADS)
            for t in range(NT):
                for s in range(2):
                    max_scores(0, 0, t, s, first=True)
            transpose_max(0)
            with pe.Fori(0, G // NBUF) as i:
                for u in range(NBUF):
                    head(i * NBUF + u, u, i + 1 if u < NBUF - 1 else i + 2, True)
            for g in range(G // NBUF * NBUF, G):
                head(g, g % NBUF, (g + 1) // NBUF + 1, g + 1 < G)

            def project(n):
                pe.wait_ge(oT_lo, (n + 1) * KC)
                for t in range(TT):
                    if t < 2:
                        pe.wait_ge(h2_hi, START + n * KC)
                    else:
                        pe.wait_ge(o_tmp, n * TT + t - 1)
                    product(ps[:, t % 2, :], lambda s, kk: oT_r[:, s, kk, t * P:(t + 1) * P],
                            lambda s, kk: wo_r[:, s, kk, :]).then_inc(o_mm, 1)

            def mlp1(n, f):
                if f >= 2:
                    pe.wait_ge(gelu_ok, START + n * FB + f - 1)
                else:
                    pe.wait_ge(gelu_ok, START + n * FB)
                product(ps[:, 2 + f % 2, :], lambda s, kk: w1_r[:, s, kk, f * P:(f + 1) * P],
                        lambda s, kk: h2T[:, s, kk, :]).then_inc(m1_mm, 1)

            def mlp2(n, f):
                pe.wait_ge(g_lo, START + n * FB + f + 1)
                if f == 0:
                    pe.wait_ge(y_ok, START + n * TT)
                for t in range(TT):
                    for s, r in ((0, 0), (0, 1), (1, 0)):
                        mm = nc.tensor.matmul(ps[:, 4 + t, :], g_r[:, f % 4, s, t * P:(t + 1) * P], w2_r[:, r, f, :],
                                              start=(f == 0 and s == r), stop=(f == FB - 1 and s == 1))
                mm.then_inc(m2_used, 1)

            def stage3(c, b, nxt):
                n = c * 2 + b
                pe.wait_ge(o_tmp, (n + 1) * TT)
                transposes(n, xn3, xn3_ok, h2_hi, h2_mm)
                if nxt:
                    pe.wait_ge(h2_hi, START + (n + 1) * KC)
                    project(n + 1)
                pe.wait_ge(h2_lo, START + (n + 1) * KC)
                mlp1(n, 0)
                mlp1(n, 1)
                for f in range(FB):
                    mlp2(n, f)
                    if f + 2 < FB:
                        mlp1(n, f + 2)

            pe.wait_ge(w_lo, 8)
            pe.wait_ge(o_ok, START + G)
            project(0)
            with pe.Fori(0, CPB - 1) as c:
                for b in range(2):
                    stage3(c, b, True)
            stage3(CPB - 1, 0, True)
            stage3(CPB - 1, 1, False)


def kernel(x, cond_1024, L0_cond_Wq, L0_cond_bq, L0_cond_Wk, L0_cond_bk, L0_cond_Wv, L0_cond_bv, L0_cond_Wo,
           L0_cond_bo, L0_cond_W1, L0_cond_b1, L0_cond_W2, L0_cond_b2, L0_cond_Wada, L0_cond_bada):
    import numpy as np
    import concourse.bacc as bacc
    from concourse.bass_utils import run_bass_kernel_spmd

    def columns(a):
        a = np.asarray(a)
        return np.ascontiguousarray(a.reshape(-1, P).T)

    c = np.asarray(cond_1024)
    inputs = {
        "x": np.asarray(x),
        "cT": np.ascontiguousarray(c.reshape(B, KC, P).transpose(2, 1, 0)),
        "wq": L0_cond_Wq, "wk": L0_cond_Wk, "wv": L0_cond_Wv, "wo": L0_cond_Wo, "w1": L0_cond_W1, "w2": L0_cond_W2,
        "wada": L0_cond_Wada, "bqT": columns(L0_cond_bq), "bkT": columns(L0_cond_bk), "b1T": columns(L0_cond_b1),
        "badaT": np.ascontiguousarray(columns(L0_cond_bada).reshape(P, 6, KC)), "bada": L0_cond_bada,
        "bv": L0_cond_bv, "bo": L0_cond_bo, "b2": L0_cond_b2,
    }
    nc = bacc.Bacc("TRN2", target_bir_lowering=False, num_devices=1)
    arrays, args = {}, []
    for name, a in inputs.items():
        a = np.ascontiguousarray(np.asarray(a))
        arrays[f"in_{name}"] = a
        args.append(nc.dram_tensor(f"in_{name}", a.shape, mybir.dt.from_np(a.dtype), kind="ExternalInput").ap())
    out = nc.dram_tensor("out_y", (B, L, D), F32, kind="ExternalOutput").ap()
    block_kernel(nc, *args, out)
    r = run_bass_kernel_spmd(nc, [arrays], core_ids=[0])
    return r.results[0]["out_y"]
```

```python
from contextlib import ExitStack

import concourse.bass as bass
from concourse import mybir

F32 = mybir.dt.float32
F32R = mybir.dt.float32r
ALU = mybir.AluOpType
ACT = mybir.ActivationFunctionType
AX = mybir.AxisListType

P = 128
B, L, D, H = 2, 2048, 512, 16
DH = D // H
FF = 2 * D
EPS = 1e-6
SCALE = float(DH) ** -0.5
KC = D // P
FB = FF // P
CH = 512
TT = CH // P
CPB = L // CH
NCHUNK = B * CPB
G = B * H
NT = L // P
NQ = L // CH
MIX = D // DH
RING = 4
NBUF = 3
M_ROW = 3 * DH
POOL_TILES = [0, 1, 3, 4, 6, 7, 9, 10, 12, 13]
PE_TILES = [t for t in range(NT) if t not in POOL_TILES]
NADD = len(POOL_TILES) - 1
FILLS = NQ * NT
LONG_STEPS = (1, 3, 6, 9)
A_BANKS, B_BANKS = 3, 3
O_BANK, DEN_BANK = 6, 7
START = 1
LOADS = 7


def block_kernel(nc, x, cT, wq, wk, wv, wo, w1, w2, wada, bqT, bkT, b1T, badaT, bada, bv, bo, b2, out):
    qk_hi = [nc.dram_tensor(f"{n}_hi", [B * D, L], F32, kind="Internal").ap() for n in "qk"]
    qk_lo = [nc.dram_tensor(f"{n}_lo", [B * D, L], F32, kind="Internal").ap() for n in "qk"]
    v_dram = nc.dram_tensor("v_rows", [L, B * D], F32, kind="Internal").ap()
    att_dram = nc.dram_tensor("attention_T", [D, B * L], F32, kind="Internal").ap()

    with ExitStack() as ctx:
        def sb(name, shape, dt=F32):
            return ctx.enter_context(nc.sbuf_tensor(name, shape, dt))

        def sem(name):
            return ctx.enter_context(nc.semaphore(name))

        weights_r = sb("weights_r", [P, 12288], F32R)
        w2_r = sb("w2_r", [P, 2, FB, D], F32R)
        acts_r = sb("acts_r", [P, 12288], F32R)
        work = sb("work", [P, 13312])
        ps = ctx.enter_context(nc.psum_tensor("ps", [P, 8, 512], F32))

        def view(t, at, *shape):
            n = 1
            for s in shape:
                n *= s
            ap = t[:, at:at + n]
            names = "abcd"[:len(shape)]
            if len(shape) == 1:
                return ap
            return ap.rearrange(f"p ({' '.join(names)}) -> p {' '.join(names)}",
                                **{k: s for k, s in zip(names[1:], shape[1:])})

        wqkv = view(weights_r, 0, 2, KC, 3 * D)
        wo_r = view(weights_r, 0, 2, KC, D)
        w1_r = view(weights_r, 2 * KC * D, 2, KC, FF)
        hT = [view(acts_r, b * 2 * KC * CH, 2, KC, CH) for b in range(2)]
        qs = [view(acts_r, 4096 * u, L) for u in range(NBUF)]
        ks = [view(acts_r, 4096 * u + L, L) for u in range(NBUF)]
        oT_r = view(acts_r, 0, 2, KC, CH)
        h2T = view(acts_r, 2 * KC * CH, 2, KC, CH)
        g_r = view(acts_r, 4 * KC * CH, 4, 2, CH)

        x1c = [view(work, 2048 * b, TT, D) for b in range(2)]
        hTf1 = view(work, 4096, KC, CH)
        qk_st = view(work, 6144, 2, 2, CH)
        v_st = view(work, 8192, 2, D)
        stage = [view(work, 9216 + 2048 * s, KC, D) for s in range(2)]
        v_sb = [view(work, 512 * u, NT, DH) for u in range(NBUF)]
        psum_acc = view(work, 1536, L)
        o_st = [view(work, 3584 + 512 * u, CH) for u in range(NBUF)]
        prob = view(work, 5120, RING, L)
        xc = [view(work, 2048 * b, TT, D) for b in range(2)]
        xn3 = view(work, 4096, TT, D)
        oTf = [view(work, 6144 + 2048 * b, KC, CH) for b in range(2)]
        hTf3 = view(work, 10240, KC, CH)
        gf = view(work, 12288, 2, CH)

        tmp3 = sb("tmp3", [P, 2, D])
        gate = sb("gate", [P, 2, B, D])
        gate_b = sb("gate_b", [P, 2, B, D])
        bv_rows = sb("bv_rows", [P, D])
        mod = sb("mod", [P, 4, KC, B])
        ident = sb("ident", [P, P])
        ones = sb("ones", [P, P])
        recip = sb("recip", [P, CH])
        c_sb = sb("c_sb", [P, KC, B])
        cs = sb("cs", [P, KC, B])
        bq_sb = sb("bq_sb", [P, 2, KC])
        b1_sb = sb("b1_sb", [P, FB])
        bada_sb = sb("bada_sb", [P, 6, KC])
        stats = sb("stats", [P, TT, 6])
        mv = sb("mv", [P, TT, 2])
        var_eps = sb("var_eps", [P, TT])
        minus_half = sb("minus_half", [P, TT])
        rstd = sb("rstd", [P, TT])
        part_max = sb("part_max", [P, NT, NQ])
        row_max = sb("row_max", [P, NT])
        neg_max = sb("neg_max", [NT, P], F32R)
        cs_wide = view(work, 4096, KC, B, P)
        bias_wide = view(work, 6144, 2, D)
        bias_rows = view(work, 7168, 3, D)[0:1]
        gate_rows = view(work, 5120, 2, D)[0:1]

        consts_in = sem("consts_in")
        staged = [sem(f"staged{s}") for s in range(2)]
        ident_ok = sem("ident_ok")
        ones_ok = sem("ones_ok")
        silu_ok = sem("silu_ok")
        wide_ok = sem("wide_ok")
        ada_mm = sem("ada_mm")
        mod_ok = sem("mod_ok")
        bias_mm = sem("bias_mm")
        bias_ok = sem("bias_ok")
        gateb_ok = sem("gateb_ok")
        w_hi = sem("w_hi")
        w_lo = sem("w_lo")

        x_in = [sem(f"x_in{b}") for b in range(2)]
        stats_ok = sem("stats_ok")
        mv_ok = sem("mv_ok")
        eps_ok = sem("eps_ok")
        rstd_ok = sem("rstd_ok")
        xn_ok = sem("xn_ok")
        xT_mm = sem("xT_mm")
        hT_hi = sem("hT_hi")
        hT_lo = sem("hT_lo")
        qkv_mm = sem("qkv_mm")
        qk_hi_ok = sem("qk_hi_ok")
        qk_lo_ok = sem("qk_lo_ok")
        v_ok = sem("v_ok")
        qk_out = [sem(f"qk_out{s}") for s in range(2)]
        v_out = [sem(f"v_out{s}") for s in range(2)]

        ones_row = sem("ones_row")
        head_in = [sem(f"head_in{u}") for u in range(NBUF)]
        a_mm = sem("a_mm")
        a_max = sem("a_max")
        max_ok = sem("max_ok")
        maxT_mm = sem("maxT_mm")
        neg_ok = sem("neg_ok")
        neg_in = sem("neg_in")
        b_mm = sem("b_mm")
        exp_ok = sem("exp_ok")
        pv_mm = sem("pv_mm")
        add_ok = sem("add_ok")
        den_mm = sem("den_mm")
        o_raw = sem("o_raw")
        den_raw = sem("den_raw")
        rec_ok = sem("rec_ok")
        o_ok = sem("o_ok")
        o_out = [sem(f"o_out{u}") for u in range(NBUF)]

        xc_in = [sem(f"xc_in{b}") for b in range(2)]
        oT_in = [sem(f"oT_in{b}") for b in range(2)]
        oT_hi = sem("oT_hi")
        oT_lo = sem("oT_lo")
        o_mm = sem("o_mm")
        xg_ok = sem("xg_ok")
        o_tmp = sem("o_tmp")
        x1_ok = sem("x1_ok")
        stats3 = sem("stats3")
        mv3 = sem("mv3")
        eps3 = sem("eps3")
        rstd3 = sem("rstd3")
        xn3_ok = sem("xn3_ok")
        h2_mm = sem("h2_mm")
        h2_hi = sem("h2_hi")
        h2_lo = sem("h2_lo")
        m1_mm = sem("m1_mm")
        gelu_ok = sem("gelu_ok")
        g_hi = sem("g_hi")
        g_lo = sem("g_lo")
        m2_used = sem("m2_used")
        x1g_ok = sem("x1g_ok")
        m2_tmp = sem("m2_tmp")
        y_ok = sem("y_ok")
        y_out = [sem(f"y_out{b}") for b in range(2)]

        start_at_one = [pv_mm, add_ok, m1_mm, hT_lo, h2_lo, g_lo, m2_used, y_ok, hT_hi, h2_hi, v_ok, exp_ok, o_ok, gelu_ok, den_mm,
                        *v_out, *o_out]

        block = ctx.enter_context(nc.Block())

        def rows_of(w, c0):
            return w[:, c0:c0 + D].rearrange("(k p) n -> p k n", p=P)

        early = [("ada", n, rows_of(wada, n * D)) for n in (0, 1)]
        early += [("w", n, rows_of(w, 0)) for n, w in enumerate((wq, wk, wv))]
        early += [("ada", n, rows_of(wada, n * D)) for n in (2, 3, 4, 5)]
        early += [("w", 3 + n, w2[n * D:(n + 1) * D, :].rearrange("(k p) n -> p k n", p=P)) for n in range(2)]
        late = [("w", 5, rows_of(wo, 0)), ("w", 6, rows_of(w1, 0)), ("w", 7, rows_of(w1, D))]
        pieces = early + late
        ADA_ORDER = [n for kind, n, _ in pieces if kind == "ada"]
        N_CONST = 10

        def split_of(n):
            if n < 3:
                return [wqkv[:, s, :, n * D:(n + 1) * D] for s in range(2)]
            if n < 5:
                return [w2_r[:, s, (n - 3) * KC:(n - 2) * KC, :] for s in range(2)]
            if n == 5:
                return [wo_r[:, s] for s in range(2)]
            return [w1_r[:, s, :, (n - 6) * D:(n - 5) * D] for s in range(2)]

        MM_CHUNK = 2 * KC + TT
        MOD_SHIFT1, MOD_SCALE1, MOD_SHIFT2, MOD_SCALE2 = range(4)
        MOD_OF = {0: MOD_SHIFT1, 1: MOD_SCALE1, 3: MOD_SHIFT2, 4: MOD_SCALE2}
        GATE_OF = {2: 0, 5: 1}

        @block.sync
        def _(sp):
            for s in start_at_one:
                sp.sem_inc(s, START)

            def load_x(b, c, dst, s):
                sp.dma_start(dst[b], x[b, bass.ds(c * CH, CH), :].rearrange("(t p) d -> p t d", p=P)).then_inc(s[b], 16)

            def load_x_mixed(b, c):
                sp.dma_start(x1c[b], x[b].rearrange("(p r) d -> p r d", r=MIX)[:, bass.ds(c * TT, TT), :]).then_inc(x_in[b], 16)

            def load_piece(k):
                if k >= 2:
                    kind, n, _ = pieces[k - 2]
                    if kind == "ada":
                        sp.wait_ge(ada_mm, ADA_ORDER.index(n) + 1)
                    else:
                        sp.wait_ge(w_hi, n + 1)
                        sp.wait_ge(w_lo, n + 1)
                sp.dma_start(stage[k % 2], pieces[k][2]).then_inc(staged[k % 2], 16)

            sp.dma_start(c_sb[:], cT).then_inc(consts_in, 16)
            load_piece(0)
            load_piece(1)
            load_x_mixed(0, 0)
            load_x_mixed(1, 0)
            sp.dma_start(bq_sb[:, 0, :], bqT).then_inc(consts_in, 16)
            sp.dma_start(bq_sb[:, 1, :], bkT).then_inc(consts_in, 16)
            sp.dma_start(b1_sb[:], b1T).then_inc(consts_in, 16)
            sp.dma_start(bada_sb[:], badaT).then_inc(consts_in, 16)
            for n, r in enumerate((bv, bo, b2)):
                sp.dma_start(bias_rows[:, n, :], r.rearrange("(o d) -> o d", o=1)).then_inc(consts_in, 16)
            for n, r in enumerate((bada[2 * D:3 * D], bada[5 * D:6 * D])):
                sp.dma_start(gate_rows[:, n, :], r.rearrange("(o d) -> o d", o=1)).then_inc(consts_in, 16)
            for k in range(2, len(early)):
                load_piece(k)

            def store_qkv(c, b, n):
                for m in range(2 * KC):
                    t, blk = m // KC, m % KC
                    at = slice(b * D + blk * P, b * D + (blk + 1) * P)
                    sp.wait_ge(qk_lo_ok, n * 2 * KC + m + 1)
                    sp.dma_start(qk_hi[t][at, bass.ds(c * CH, CH)], qk_st[:, m % 2, 0, :]).then_inc(qk_out[m % 2], 16)
                    sp.dma_start(qk_lo[t][at, bass.ds(c * CH, CH)], qk_st[:, m % 2, 1, :]).then_inc(qk_out[m % 2], 16)
                for t in range(TT):
                    sp.wait_ge(v_ok, START + n * TT + t + 1)
                    sp.dma_start(v_dram[bass.ds(c * CH + t * P, P), b * D:(b + 1) * D], v_st[:, t % 2, :]).then_inc(v_out[t % 2], 16)

            def stage1(c, b, more):
                n = c * 2 + b
                if more:
                    sp.wait_ge(xT_mm, n * KC + KC)
                    load_x_mixed(b, c + 1)
                store_qkv(c, b, n)

            with sp.Fori(0, CPB - 1) as c:
                for b in range(2):
                    stage1(c, b, True)
            for b in range(2):
                stage1(CPB - 1, b, False)

            for k in range(len(early), len(pieces)):
                load_piece(k)

            for s in range(2):
                sp.wait_ge(qk_out[s], 16 * 2 * NCHUNK * KC)
                sp.wait_ge(v_out[s], START + 16 * NCHUNK * TT // 2)

            def load_head(g, u):
                r = bass.ds(g * DH, DH)
                for blk, (q, k) in enumerate(((qk_hi, qk_hi), (qk_hi, qk_lo), (qk_lo, qk_hi))):
                    at = slice(blk * DH, (blk + 1) * DH)
                    sp.dma_start(qs[u][at, :].bitcast(F32), q[0][r, :]).then_inc(head_in[u], 16)
                    sp.dma_start(ks[u][at, :].bitcast(F32), k[1][r, :]).then_inc(head_in[u], 16)
                sp.dma_start(v_sb[u], v_dram[:, r].rearrange("(t p) d -> p t d", p=P)).then_inc(head_in[u], 16)

            def put_max(g, u):
                sp.wait_ge(neg_ok, g + 1)
                sp.dma_start(qs[u][M_ROW:M_ROW + 1, :].bitcast(F32),
                             neg_max[:].bitcast(F32)).then_inc(neg_in, 16)

            def store_head(g, u):
                sp.wait_ge(o_ok, START + g + 1)
                for j in range(NQ):
                    sp.dma_start(att_dram[j * P:(j + 1) * P, bass.ds(g * P, P)].rearrange("(r d) q -> d r q", d=DH),
                                 o_st[u][j * DH:(j + 1) * DH, :].rearrange("d (r q) -> d r q", q=P)).then_inc(o_out[u], 16)

            def stage2(g, u, load):
                if load:
                    sp.wait_ge(den_mm, START + g)
                    load_head(g + 2, (u + 2) % NBUF)
                put_max(g + 1, (u + 1) % NBUF)
                store_head(g - 1, (u + 2) % NBUF)

            load_head(0, 0)
            load_head(1, 1)
            put_max(0, 0)
            load_head(2, 2)
            put_max(1, 1)
            with sp.Fori(0, G // NBUF - 1) as i:
                for k in range(1, NBUF + 1):
                    stage2(i * NBUF + k, k % NBUF, True)
            for g in range(G // NBUF * NBUF - NBUF + 1, G - 1):
                stage2(g, g % NBUF, g + 2 < G)
            for g in range(G - 2, G):
                store_head(g, g % NBUF)
            for u in range(NBUF):
                sp.wait_ge(o_out[u], START + 16 * NQ * len(range(u, G, NBUF)))

            def load_oT(b, c):
                sp.dma_start(oTf[b], att_dram[:, bass.ds(b * L + c * CH, CH)].rearrange("(k p) q -> p k q", p=P)).then_inc(oT_in[b], 16)

            for b in range(2):
                load_x(b, 0, xc, xc_in)
                load_oT(b, 0)

            def stage3(c, b, more):
                n = c * 2 + b
                if more:
                    sp.wait_ge(oT_lo, (n + 1) * KC)
                    sp.wait_ge(oT_hi, (n + 1) * KC)
                    load_oT(b, c + 1)
                sp.wait_ge(y_ok, START + (n + 1) * TT)
                sp.dma_start(out[b, bass.ds(c * CH, CH), :].rearrange("(t p) d -> p t d", p=P), xc[b]).then_inc(y_out[b], 16)
                if more:
                    sp.wait_ge(y_out[b], c * 16 + 16)
                    load_x(b, c + 1, xc, xc_in)

            with sp.Fori(0, CPB - 1) as c:
                for b in range(2):
                    stage3(c, b, True)
            for b in range(2):
                stage3(CPB - 1, b, False)
            for b in range(2):
                sp.wait_ge(y_out[b], 16 * CPB)

        @block.gpsimd
        def _(pool):
            nc.gpsimd.memset(ident[:], 0.0).then_inc(ident_ok, 1)
            pool.wait_ge(ident_ok, 1)
            nc.gpsimd.affine_select(out=ident[:], in_=ident[:], compare_op=ALU.not_equal, fill=1.0, base=0,
                                    pattern=[[-1, P]], channel_multiplier=1).then_inc(ident_ok, 1)
            nc.gpsimd.memset(minus_half[:], -0.5).then_inc(ident_ok, 1)
            pool.wait_ge(ident_ok, 3)

            def root(n, wait, added, done):
                pool.wait_ge(wait, (n + 1) * TT)
                nc.gpsimd.tensor_tensor(var_eps[:], var_eps[:], mv[:, :, 1], ALU.add).then_inc(added, 1)
                pool.wait_ge(added, n + 1)
                nc.gpsimd.tensor_tensor(rstd[:], var_eps[:], minus_half[:], ALU.pow).then_inc(done, 1)

            with pool.Fori(0, NCHUNK) as n:
                root(n, mv_ok, eps_ok, rstd_ok)

            def sum_probs(g):
                pool.wait_ge(den_mm, START + g)
                for k in range(NADD):
                    t = POOL_TILES[k + 1]
                    pool.wait_ge(exp_ok, START + g * (NT * NQ) + (t + 1) * NQ)
                    if k:
                        pool.wait_ge(add_ok, START + g * NADD + k)
                    first = prob[:, POOL_TILES[0] % RING, :] if k == 0 else psum_acc
                    nc.gpsimd.tensor_tensor(psum_acc, first, prob[:, t % RING, :], ALU.add).then_inc(add_ok, 1)

            with pool.Fori(0, G) as g:
                sum_probs(g)

            def add_bias(n, b, which, waits, done):
                for s, v in waits:
                    pool.wait_ge(s, v)
                for t in range(TT):
                    nc.gpsimd.tensor_tensor(xc[b][:, t, :], xc[b][:, t, :], gate_b[:, which, b, :], ALU.add).then_inc(done, 1)

            add_bias(0, 0, 0, [(xc_in[0], 16), (gateb_ok, 4)], xg_ok)
            root(0, mv3, eps3, rstd3)

            def stage3(c, b, nxt):
                n = c * 2 + b
                if nxt:
                    add_bias(n + 1, 1 - b, 0, [(xc_in[1 - b], (c + b) * 16 + 16)], xg_ok)
                add_bias(n, b, 1, [(xn3_ok, (n + 1) * TT)], x1g_ok)
                if nxt:
                    root(n + 1, mv3, eps3, rstd3)

            with pool.Fori(0, CPB - 1) as c:
                for b in range(2):
                    stage3(c, b, True)
            stage3(CPB - 1, 0, True)
            stage3(CPB - 1, 1, False)

        @block.scalar
        def _(act):
            act.wait_ge(consts_in, 16 * N_CONST)
            nc.scalar.activation(cs[:], c_sb[:], ACT.Silu).then_inc(silu_ok, 1)

            def split_hi(k):
                kind, n, _ = pieces[k]
                if kind == "w":
                    act.wait_ge(staged[k % 2], 16 * (k // 2 + 1))
                    nc.scalar.activation(split_of(n)[0], stage[k % 2], ACT.Copy).then_inc(w_hi, 1)

            for k in range(len(early)):
                split_hi(k)

            def modulate(n, b, xT, wait, used, hTf, h, shift, scale, done):
                for blk in range(KC):
                    act.wait_ge(wait, n * KC + blk + 1)
                    if used is not None:
                        act.wait_ge(used, START + n * KC)
                    kw = dict(scale=mod[:, scale, blk, b:b + 1], bias=mod[:, shift, blk, b:b + 1])
                    nc.scalar.activation(h[:, 0, blk, :], ps[:, xT + blk % 2, :], ACT.Identity, **kw)
                    nc.scalar.activation(hTf[:, blk, :], ps[:, xT + blk % 2, :], ACT.Identity, **kw).then_inc(done, 1)

            def hT1(c, b):
                n = c * 2 + b
                if not (isinstance(n, int) and n < 2):
                    act.wait_ge(qkv_mm, (n - 1) * MM_CHUNK)
                modulate(n, b, 0, xT_mm, hT_lo, hTf1, hT[b], MOD_SHIFT1, MOD_SCALE1, hT_hi)

            def heads_of_qk(c, b):
                n = c * 2 + b
                for m in range(2 * KC):
                    act.wait_ge(qkv_mm, n * MM_CHUNK + m + 1)
                    if not (isinstance(n, int) and n == 0 and m < 2):
                        act.wait_ge(qk_out[m % 2], (n * KC + m // 2) * 32)
                    nc.scalar.activation(qk_st[:, m % 2, 0, :].bitcast(F32R), ps[:, 2 + m % 4, :], ACT.Identity,
                                         bias=bq_sb[:, m // KC, m % KC:m % KC + 1]).then_inc(qk_hi_ok, 1)

            act.wait_ge(mod_ok, 6)
            act.wait_ge(gateb_ok, 4)
            hT1(0, 0)
            hT1(0, 1)
            heads_of_qk(0, 0)
            with act.Fori(1, CPB) as c:
                hT1(c, 0)
                heads_of_qk(c - 1, 1)
                hT1(c, 1)
                heads_of_qk(c, 0)
            heads_of_qk(CPB - 1, 1)

            act.wait_ge(qkv_mm, NCHUNK * MM_CHUNK)
            for k in range(len(early), len(pieces)):
                split_hi(k)
            act.wait_ge(w_lo, 8)

            def take_output(g, u, uses):
                act.wait_ge(pv_mm, START + (g + 1) * NT)
                act.wait_ge(o_out[u], START + uses * (16 * NQ))
                nc.scalar.activation(o_st[u], ps[:, O_BANK, :], ACT.Copy).then_inc(o_raw, 1)

            def take_denominator(g):
                act.wait_ge(den_mm, START + g + 1)
                act.wait_ge(o_ok, START + g)
                nc.scalar.activation(recip[:], ps[:, DEN_BANK, :], ACT.Copy).then_inc(den_raw, 1)

            def probs(g, u, uses, prev):
                for t in range(NT):
                    last, gl = ((t - RING) % NT, g if t >= RING else g - 1)
                    if t >= RING or prev:
                        act.wait_ge(pv_mm, START + gl * NT + last + 1)
                        if last in POOL_TILES:
                            act.wait_ge(add_ok, START + gl * NADD + max(POOL_TILES.index(last), 1))
                    for j in range(NQ):
                        act.wait_ge(b_mm, g * (NT * NQ) + t * NQ + j + 1)
                        nc.scalar.activation(prob[:, t % RING, j * CH:(j + 1) * CH], ps[:, A_BANKS + (u + t * NQ + j) % B_BANKS, :],
                                             ACT.Exp, scale=SCALE).then_inc(exp_ok, 1)
                    if prev and t == 0:
                        take_output(g - 1, (u + 2) % NBUF, uses)
                    if prev and t == 1:
                        take_denominator(g - 1)

            probs(0, 0, 0, False)
            with act.Fori(0, G // NBUF) as i:
                for k in range(1, NBUF + 1):
                    probs(i * NBUF + k, k % NBUF, i, True)
            probs(G - 1, (G - 1) % NBUF, (G - 2) // NBUF, True)
            take_output(G - 1, (G - 1) % NBUF, (G - 1) // NBUF)
            take_denominator(G - 1)

            def split_oT(n, b, c):
                act.wait_ge(oT_in[b], c * 16 + 16)
                if not isinstance(n, int) or n:
                    act.wait_ge(o_mm, n * TT)
                for blk in range(KC):
                    nc.scalar.activation(oT_r[:, 0, blk, :], oTf[b][:, blk, :], ACT.Copy).then_inc(oT_hi, 1)

            split_oT(0, 0, 0)

            def stage3(c, b, nxt):
                n = c * 2 + b
                if nxt:
                    split_oT(n + 1, 1 - b, c + b)
                act.wait_ge(m1_mm, START + n * FB)
                modulate(n, b, 0, h2_mm, h2_lo, hTf3, h2T, MOD_SHIFT2, MOD_SCALE2, h2_hi)
                for f in range(FB):
                    act.wait_ge(m1_mm, START + n * FB + f + 1)
                    if f >= 2:
                        act.wait_ge(g_lo, START + n * FB + f - 1)
                    else:
                        act.wait_ge(g_lo, START + n * FB)
                    nc.scalar.activation(gf[:, f % 2, :], ps[:, 2 + f % 2, :], ACT.Gelu, bias=b1_sb[:, f:f + 1]).then_inc(gelu_ok, 1)

            with act.Fori(0, CPB - 1) as c:
                for b in range(2):
                    stage3(c, b, True)
            stage3(CPB - 1, 0, True)
            stage3(CPB - 1, 1, False)

        @block.vector
        def _(dve):
            nc.vector.memset(ones[:], 1.0).then_inc(ones_ok, 1)
            dve.wait_ge(ones_ok, 1)
            dve.wait_ge(silu_ok, 1)
            for k in range(KC):
                for b in range(B):
                    nc.vector.tensor_scalar(cs_wide[:, k, b, :], ones[:], cs[:, k, b:b + 1], None, ALU.mult).then_inc(wide_ok, 1)

            def split_lo(k):
                kind, n, _ = pieces[k]
                if kind == "w":
                    dve.wait_ge(w_hi, n + 1)
                    hi, lo = split_of(n)
                    nc.vector.tensor_tensor(lo, stage[k % 2], hi.bitcast(F32), ALU.subtract).then_inc(w_lo, 1)

            def take_ada(n):
                at = ADA_ORDER.index(n)
                dve.wait_ge(ada_mm, at + 1)
                if n in MOD_OF:
                    for b in range(B):
                        ins = nc.vector.scalar_tensor_tensor(
                            out=mod[:, MOD_OF[n], :, b], in0=ps[:, 6, 0:KC * B].rearrange("p (k b) -> p k b", b=B)[:, :, b],
                            scalar=1.0 if n in (1, 4) else 0.0, in1=bada_sb[:, n, :], op0=ALU.add, op1=ALU.add)
                else:
                    for b in range(B):
                        ins = nc.vector.tensor_copy(gate[:, GATE_OF[n], b, :], ps[:, 6 + b, :])
                ins.then_inc(mod_ok, 1)

            for k in range(3):
                dve.wait_ge(bias_mm, k + 1)
                nc.vector.tensor_copy(bv_rows[:] if k == 0 else bias_wide[:, k - 1, :], ps[:, k, :]).then_inc(bias_ok, 1)
            for k, (kind, n, _) in enumerate(early):
                if kind == "ada":
                    take_ada(n)
                else:
                    split_lo(k)
            dve.wait_ge(bias_ok, 3)
            dve.wait_ge(mod_ok, 6)
            for w in range(2):
                for b in range(B):
                    nc.vector.tensor_tensor(gate_b[:, w, b, :], gate[:, w, b, :], bias_wide[:, w, :], ALU.mult).then_inc(gateb_ok, 1)

            def norm_stats(n, src, ok):
                for t in range(TT):
                    nc.vector.bn_stats(stats[:, t, :], src[:, t, :]).then_inc(ok, 1)

            def norm_mean(n, ok, done):
                dve.wait_ge(ok, (n + 1) * TT)
                nc.vector.memset(var_eps[:], EPS)
                for t in range(TT):
                    nc.vector.bn_aggr(mv[:, t, :], stats[:, t, :]).then_inc(done, 1)

            def norm_apply(n, src, dst, ok, done):
                dve.wait_ge(ok, n + 1)
                for t in range(TT):
                    nc.vector.tensor_scalar(dst[:, t, :], src[:, t, :], mv[:, t, 0:1], rstd[:, t:t + 1],
                                            ALU.subtract, ALU.mult).then_inc(done, 1)

            def norm1(c, b):
                n = c * 2 + b
                dve.wait_ge(x_in[b], c * 16 + 16)
                if not (isinstance(n, int) and n == 0):
                    dve.wait_ge(xn_ok, n * TT)
                norm_stats(n, x1c[b], stats_ok)
                norm_mean(n, stats_ok, mv_ok)
                norm_apply(n, x1c[b], x1c[b], rstd_ok, xn_ok)

            def remainders(n, hi_ok, hTf, h, done):
                for blk in range(KC):
                    dve.wait_ge(hi_ok, START + n * KC + blk + 1)
                    nc.vector.tensor_tensor(h[:, 1, blk, :], hTf[:, blk, :], h[:, 0, blk, :].bitcast(F32), ALU.subtract).then_inc(done, 1)

            def take_qkv(c, b):
                n = c * 2 + b
                for m in range(2 * KC):
                    dve.wait_ge(qk_hi_ok, n * 2 * KC + m + 1)
                    nc.vector.scalar_tensor_tensor(
                        out=qk_st[:, m % 2, 1, :].bitcast(F32R), in0=ps[:, 2 + m % 4, :], scalar=bq_sb[:, m // KC, m % KC:m % KC + 1],
                        in1=qk_st[:, m % 2, 0, :], op0=ALU.add, op1=ALU.subtract).then_inc(qk_lo_ok, 1)
                for t in range(TT):
                    dve.wait_ge(qkv_mm, n * MM_CHUNK + 2 * KC + t + 1)
                    dve.wait_ge(v_out[t % 2], START + (n * (TT // 2) + t // 2) * 16)
                    nc.vector.tensor_tensor(v_st[:, t % 2, :], ps[:, 2 + t % 4, :], bv_rows[:], ALU.add).then_inc(v_ok, 1)

            norm1(0, 0)
            norm1(0, 1)
            remainders(0, hT_hi, hTf1, hT[0], hT_lo)
            with dve.Fori(0, CPB - 1) as c:
                remainders(c * 2 + 1, hT_hi, hTf1, hT[1], hT_lo)
                norm1(c + 1, 0)
                take_qkv(c, 0)
                remainders(c * 2 + 2, hT_hi, hTf1, hT[0], hT_lo)
                norm1(c + 1, 1)
                take_qkv(c, 1)
            remainders(NCHUNK - 1, hT_hi, hTf1, hT[1], hT_lo)
            take_qkv(CPB - 1, 0)
            take_qkv(CPB - 1, 1)

            dve.wait_ge(qkv_mm, NCHUNK * MM_CHUNK)
            for u in range(NBUF):
                nc.vector.memset(ks[u][M_ROW:M_ROW + 1, :].bitcast(F32), 1.0).then_inc(ones_row, 1)
            for k in range(len(early), len(pieces)):
                split_lo(k)

            def find_max(g, u):
                for f in range(FILLS):
                    dve.wait_ge(a_mm, g * FILLS + f + 1)
                    nc.vector.tensor_reduce(part_max[:, f // NQ, f % NQ:f % NQ + 1], ps[:, (u + f) % A_BANKS, :], AX.X, ALU.max).then_inc(a_max, 1)
                dve.wait_ge(a_max, (g + 1) * FILLS)
                nc.vector.tensor_reduce(row_max[:], part_max[:], AX.X, ALU.max).then_inc(max_ok, 1)
                dve.wait_ge(maxT_mm, g + 1)
                if not isinstance(g, int) or g:
                    dve.wait_ge(neg_in, g * 16)
                nc.vector.tensor_scalar(neg_max[:], ps[0:NT, 0, 0:P], -1.0, None, ALU.mult).then_inc(neg_ok, 1)

            def normalise(g, u):
                dve.wait_ge(den_raw, g + 1)
                nc.vector.reciprocal(recip[:], recip[:]).then_inc(rec_ok, 1)
                dve.wait_ge(o_raw, g + 1)
                dve.wait_ge(rec_ok, g + 1)
                nc.vector.tensor_tensor(o_st[u], o_st[u], recip[:], ALU.mult).then_inc(o_ok, 1)

            find_max(0, 0)
            find_max(1, 1)
            with dve.Fori(0, G // NBUF) as i:
                for k in range(1, NBUF + 1):
                    find_max(i * NBUF + k + 1, (k + 1) % NBUF)
                    normalise(i * NBUF + k - 1, (k - 1) % NBUF)
            for g in range(G - 2, G):
                normalise(g, g % NBUF)

            def oT_rest(n, b):
                for blk in range(KC):
                    dve.wait_ge(oT_hi, n * KC + blk + 1)
                    nc.vector.tensor_tensor(oT_r[:, 1, blk, :], oTf[b][:, blk, :], oT_r[:, 0, blk, :].bitcast(F32), ALU.subtract).then_inc(oT_lo, 1)

            def residual1(n, b):
                for t in range(TT):
                    dve.wait_ge(o_mm, n * TT + t + 1)
                    nc.vector.tensor_tensor(xn3[:, t, :], ps[:, t % 2, :], gate[:, 0, b, :], ALU.mult).then_inc(o_tmp, 1)
                    dve.wait_ge(xg_ok, n * TT + t + 1)
                    dve.wait_ge(o_tmp, n * TT + t + 1)
                    nc.vector.tensor_tensor(xc[b][:, t, :], xc[b][:, t, :], xn3[:, t, :], ALU.add).then_inc(x1_ok, 1)

            def stats_of(n, b):
                dve.wait_ge(x1_ok, (n + 1) * TT)
                norm_stats(n, xc[b], stats3)

            def split_gelu(n, f):
                dve.wait_ge(gelu_ok, START + n * FB + f + 1)
                if f >= 4:
                    dve.wait_ge(m2_used, START + n * FB + f - 3)
                else:
                    dve.wait_ge(m2_used, START + n * FB)
                nc.vector.tensor_copy(g_r[:, f % 4, 0, :], gf[:, f % 2, :]).then_inc(g_hi, 1)
                dve.wait_ge(g_hi, n * FB + f + 1)
                nc.vector.tensor_tensor(g_r[:, f % 4, 1, :], gf[:, f % 2, :], g_r[:, f % 4, 0, :].bitcast(F32), ALU.subtract).then_inc(g_lo, 1)

            def residual2(n, b):
                dve.wait_ge(m2_used, START + (n + 1) * FB)
                for t in range(TT):
                    if t >= 2:
                        dve.wait_ge(y_ok, START + n * TT + t - 1)
                    else:
                        dve.wait_ge(y_ok, START + n * TT)
                    nc.vector.tensor_tensor(tmp3[:, t % 2, :], ps[:, 4 + t, :], gate[:, 1, b, :], ALU.mult).then_inc(m2_tmp, 1)
                    dve.wait_ge(m2_tmp, n * TT + t + 1)
                    dve.wait_ge(x1g_ok, n * TT + t + 1)
                    nc.vector.tensor_tensor(xc[b][:, t, :], xc[b][:, t, :], tmp3[:, t % 2, :], ALU.add).then_inc(y_ok, 1)

            oT_rest(0, 0)
            residual1(0, 0)
            stats_of(0, 0)
            norm_mean(0, stats3, mv3)
            norm_apply(0, xc[0], xn3, rstd3, xn3_ok)

            def stage3(c, b, nxt):
                n = c * 2 + b
                if nxt:
                    oT_rest(n + 1, 1 - b)
                remainders(n, h2_hi, hTf3, h2T, h2_lo)
                if nxt:
                    residual1(n + 1, 1 - b)
                split_gelu(n, 0)
                if nxt:
                    stats_of(n + 1, 1 - b)
                split_gelu(n, 1)
                if nxt:
                    norm_mean(n + 1, stats3, mv3)
                split_gelu(n, 2)
                if nxt:
                    norm_apply(n + 1, xc[1 - b], xn3, rstd3, xn3_ok)
                for f in range(3, FB):
                    split_gelu(n, f)
                residual2(n, b)

            with dve.Fori(0, CPB - 1) as c:
                for b in range(2):
                    stage3(c, b, True)
            stage3(CPB - 1, 0, True)
            stage3(CPB - 1, 1, False)

        @block.tensor
        def _(pe):
            pe.wait_ge(ones_ok, 1)
            pe.wait_ge(consts_in, 16 * N_CONST)
            for k in range(3):
                nc.tensor.matmul(ps[:, k, :], ones[0:1, :], bias_rows[:, k, :], start=True, stop=True).then_inc(bias_mm, 1)

            def ada_piece(k, n):
                pe.wait_ge(staged[k % 2], 16 * (k // 2 + 1))
                at = ADA_ORDER.index(n)
                if at:
                    pe.wait_ge(mod_ok, at)
                w = stage[k % 2]
                if n in MOD_OF:
                    for blk in range(KC):
                        for kk in range(KC):
                            mm = nc.tensor.matmul(ps[:, 6, blk * B:(blk + 1) * B], w[:, kk, blk * P:(blk + 1) * P],
                                                  cs[:, kk, :], start=(kk == 0), stop=(kk == KC - 1))
                else:
                    for b in range(B):
                        for kk in range(KC):
                            nc.tensor.matmul(ps[:, 6 + b, :], cs_wide[:, kk, b, :], w[:, kk, :], start=(kk == 0), stop=False)
                        mm = nc.tensor.matmul(ps[:, 6 + b, :], ones[0:1, :], gate_rows[:, GATE_OF[n], :], start=False, stop=True)
                mm.then_inc(ada_mm, 1)

            pe.wait_ge(silu_ok, 1)
            pe.wait_ge(wide_ok, KC * B)
            for k, (kind, n, _) in enumerate(early):
                if kind == "ada":
                    ada_piece(k, n)

            def product(o, lhs, rhs):
                for kk in range(KC):
                    for s, r in ((0, 0), (0, 1), (1, 0)):
                        mm = nc.tensor.matmul(o, lhs(s, kk), rhs(r, kk), start=(kk == 0 and s == r), stop=(kk == KC - 1 and s == 1))
                return mm

            def transposes(n, src, wait, used, done):
                pe.wait_ge(wait, (n + 1) * TT)
                for blk in range(KC):
                    pe.wait_ge(used, START + n * KC + max(blk - 1, 0))
                    for t in range(TT):
                        mm = nc.tensor.transpose(ps[:, blk % 2, t * P:(t + 1) * P], src[:, t, blk * P:(blk + 1) * P], ident[:])
                    mm.then_inc(done, 1)

            def qkv(n, b):
                h = hT[b]
                pe.wait_ge(hT_lo, START + (n + 1) * KC)
                for m in range(2 * KC):
                    if m < 4:
                        pe.wait_ge(v_ok, START + n * TT)
                    else:
                        pe.wait_ge(qk_lo_ok, n * 2 * KC + m - 3)
                    product(ps[:, 2 + m % 4, :], lambda s, kk: wqkv[:, s, kk, m * P:(m + 1) * P],
                            lambda s, kk: h[:, s, kk, :]).then_inc(qkv_mm, 1)
                for t in range(TT):
                    pe.wait_ge(qk_lo_ok, n * 2 * KC + KC + t + 1)
                    product(ps[:, 2 + t % 4, :], lambda s, kk: h[:, s, kk, t * P:(t + 1) * P],
                            lambda s, kk: wqkv[:, s, kk, 2 * D:3 * D]).then_inc(qkv_mm, 1)

            pe.wait_ge(ident_ok, 3)
            pe.wait_ge(bias_ok, 3)
            transposes(0, x1c[0], xn_ok, hT_hi, xT_mm)
            pe.wait_ge(w_lo, 5)
            with pe.Fori(0, CPB - 1) as c:
                for b in range(2):
                    transposes(c * 2 + b + 1, x1c[1 - b], xn_ok, hT_hi, xT_mm)
                    qkv(c * 2 + b, b)
            transposes(NCHUNK - 1, x1c[1], xn_ok, hT_hi, xT_mm)
            qkv(NCHUNK - 2, 0)
            qkv(NCHUNK - 1, 1)

            def max_scores(g, u, f, first=False):
                if not (first and f < A_BANKS):
                    pe.wait_ge(a_max, g * FILLS + f - A_BANKS + 1)
                j = f % NQ
                nc.tensor.matmul(ps[:, (u + f) % A_BANKS, :], qs[u][0:M_ROW, f // NQ * P:(f // NQ + 1) * P],
                                 ks[u][0:M_ROW, j * CH:(j + 1) * CH], start=True, stop=True).then_inc(a_mm, 1)

            def transpose_max(g):
                pe.wait_ge(max_ok, g + 1)
                nc.tensor.matmul(ps[0:NT, 0, 0:P], row_max[:], ident[:], start=True, stop=True).then_inc(maxT_mm, 1)

            def scores(g, u, t, j):
                if t == 0 and j == 0:
                    pe.wait_ge(neg_in, g * 16 + 16)
                if not isinstance(g, int) or g or t or j >= B_BANKS:
                    pe.wait_ge(exp_ok, START + g * (NT * NQ) + t * NQ + j - B_BANKS + 1)
                nc.tensor.matmul(ps[:, A_BANKS + (u + t * NQ + j) % B_BANKS, :], ks[u][0:M_ROW + 1, t * P:(t + 1) * P],
                                 qs[u][0:M_ROW + 1, j * CH:(j + 1) * CH], start=True, stop=True).then_inc(b_mm, 1)

            def denominators(src, first, last):
                for j in range(NQ):
                    mm = nc.tensor.matmul(ps[j * DH:(j + 1) * DH, DEN_BANK, :], ones[:, 0:DH], src(j), start=first, stop=last)
                return mm

            def values(g, u, t, between):
                pe.wait_ge(exp_ok, START + g * (NT * NQ) + (t + 1) * NQ)
                if t == 0 and not (isinstance(g, int) and g == 0):
                    pe.wait_ge(o_raw, g)
                p = prob[:, t % RING, :]
                for j in range(NQ):
                    mm = nc.tensor.matmul(ps[j * DH:(j + 1) * DH, O_BANK, :], v_sb[u][:, t, :], p[:, j * CH:(j + 1) * CH],
                                          start=(t == 0), stop=(t == NT - 1))
                if t in PE_TILES:
                    between()
                    if t == PE_TILES[0] and not (isinstance(g, int) and g == 0):
                        pe.wait_ge(den_raw, g)
                    mm = denominators(lambda j: p[:, j * CH:(j + 1) * CH], t == PE_TILES[0], False)
                mm.then_inc(pv_mm, 1)

            def finish_denominators(g):
                pe.wait_ge(add_ok, START + (g + 1) * NADD)
                denominators(lambda j: psum_acc[:, j * CH:(j + 1) * CH], False, True).then_inc(den_mm, 1)

            def head(g, u, uses_next, prev, nxt):
                un = (u + 1) % NBUF
                if nxt:
                    pe.wait_ge(head_in[un], uses_next * (16 * LOADS))
                    pe.wait_ge(neg_ok, g + 1)
                fills = iter(range(FILLS if nxt else 0))

                def fill(t, n=1):
                    if nxt and t < NT - 2:
                        for _ in range(n):
                            max_scores(g + 1, un, next(fills))

                for t in range(NT):
                    extra = lambda: fill(t, t in LONG_STEPS)
                    scores(g, u, t, 0)
                    fill(t)
                    scores(g, u, t, 1)
                    fill(t)
                    if t == 0:
                        if prev:
                            values(g - 1, (u + 2) % NBUF, NT - 1, extra)
                    else:
                        if t == 1:
                            if prev:
                                finish_denominators(g - 1)
                            extra()
                        values(g, u, t - 1, extra)
                    extra()
                    scores(g, u, t, 2)
                    fill(t)
                    scores(g, u, t, 3)
                    fill(t)
                    if nxt and t == NT - 2:
                        transpose_max(g + 1)
                assert next(fills, None) is None

            pe.wait_ge(ones_row, NBUF)
            pe.wait_ge(v_ok, START + NCHUNK * TT)
            pe.wait_ge(head_in[0], 16 * LOADS)
            for f in range(FILLS):
                max_scores(0, 0, f, first=True)
            transpose_max(0)
            head(0, 0, 1, False, True)
            nc.disable_value_cache = True
            with pe.Fori(0, G // NBUF) as i:
                for k in range(1, NBUF + 1):
                    head(i * NBUF + k, k % NBUF, i + 1 if k + 1 < NBUF else i + 2, True, True)
            nc.disable_value_cache = False
            head(G - 1, (G - 1) % NBUF, 0, True, False)
            values(G - 1, (G - 1) % NBUF, NT - 1, lambda: None)
            finish_denominators(G - 1)

            def project(n):
                pe.wait_ge(oT_lo, (n + 1) * KC)
                for t in range(TT):
                    if t < 2:
                        pe.wait_ge(h2_hi, START + n * KC)
                    else:
                        pe.wait_ge(o_tmp, n * TT + t - 1)
                    product(ps[:, t % 2, :], lambda s, kk: oT_r[:, s, kk, t * P:(t + 1) * P],
                            lambda s, kk: wo_r[:, s, kk, :]).then_inc(o_mm, 1)

            def mlp1(n, f):
                if f >= 2:
                    pe.wait_ge(gelu_ok, START + n * FB + f - 1)
                else:
                    pe.wait_ge(gelu_ok, START + n * FB)
                product(ps[:, 2 + f % 2, :], lambda s, kk: w1_r[:, s, kk, f * P:(f + 1) * P],
                        lambda s, kk: h2T[:, s, kk, :]).then_inc(m1_mm, 1)

            def mlp2(n, f):
                pe.wait_ge(g_lo, START + n * FB + f + 1)
                if f == 0:
                    pe.wait_ge(y_ok, START + n * TT)
                for t in range(TT):
                    for s, r in ((0, 0), (0, 1), (1, 0)):
                        mm = nc.tensor.matmul(ps[:, 4 + t, :], g_r[:, f % 4, s, t * P:(t + 1) * P], w2_r[:, r, f, :],
                                              start=(f == 0 and s == r), stop=(f == FB - 1 and s == 1))
                mm.then_inc(m2_used, 1)

            def stage3(c, b, nxt):
                n = c * 2 + b
                pe.wait_ge(o_tmp, (n + 1) * TT)
                transposes(n, xn3, xn3_ok, h2_hi, h2_mm)
                if nxt:
                    pe.wait_ge(h2_hi, START + (n + 1) * KC)
                    project(n + 1)
                pe.wait_ge(h2_lo, START + (n + 1) * KC)
                mlp1(n, 0)
                mlp1(n, 1)
                for f in range(FB):
                    mlp2(n, f)
                    if f + 2 < FB:
                        mlp1(n, f + 2)

            pe.wait_ge(w_lo, 8)
            pe.wait_ge(den_raw, G)
            project(0)
            with pe.Fori(0, CPB - 1) as c:
                for b in range(2):
                    stage3(c, b, True)
            stage3(CPB - 1, 0, True)
            stage3(CPB - 1, 1, False)


def kernel(x, cond_1024, L0_cond_Wq, L0_cond_bq, L0_cond_Wk, L0_cond_bk, L0_cond_Wv, L0_cond_bv, L0_cond_Wo,
           L0_cond_bo, L0_cond_W1, L0_cond_b1, L0_cond_W2, L0_cond_b2, L0_cond_Wada, L0_cond_bada):
    import numpy as np
    import concourse.bacc as bacc
    from concourse.bass_utils import run_bass_kernel_spmd

    def columns(a):
        a = np.asarray(a)
        return np.ascontiguousarray(a.reshape(-1, P).T)

    c = np.asarray(cond_1024)
    inputs = {
        "x": np.asarray(x),
        "cT": np.ascontiguousarray(c.reshape(B, KC, P).transpose(2, 1, 0)),
        "wq": L0_cond_Wq, "wk": L0_cond_Wk, "wv": L0_cond_Wv, "wo": L0_cond_Wo, "w1": L0_cond_W1, "w2": L0_cond_W2,
        "wada": L0_cond_Wada, "bqT": columns(L0_cond_bq), "bkT": columns(L0_cond_bk), "b1T": columns(L0_cond_b1),
        "badaT": np.ascontiguousarray(columns(L0_cond_bada).reshape(P, 6, KC)), "bada": L0_cond_bada,
        "bv": L0_cond_bv, "bo": L0_cond_bo, "b2": L0_cond_b2,
    }
    nc = bacc.Bacc("TRN2", target_bir_lowering=False, num_devices=1)
    arrays, args = {}, []
    for name, a in inputs.items():
        a = np.ascontiguousarray(np.asarray(a))
        arrays[f"in_{name}"] = a
        args.append(nc.dram_tensor(f"in_{name}", a.shape, mybir.dt.from_np(a.dtype), kind="ExternalInput").ap())
    out = nc.dram_tensor("out_y", (B, L, D), F32, kind="ExternalOutput").ap()
    block_kernel(nc, *args, out)
    r = run_bass_kernel_spmd(nc, [arrays], core_ids=[0])
    return r.results[0]["out_y"]
```

```python
from contextlib import ExitStack

import concourse.bass as bass
from concourse import mybir

F32 = mybir.dt.float32
F32R = mybir.dt.float32r
ALU = mybir.AluOpType
ACT = mybir.ActivationFunctionType
AX = mybir.AxisListType

P = 128
B, L, D, H = 2, 2048, 512, 16
DH = D // H
FF = 2 * D
EPS = 1e-6
SCALE = float(DH) ** -0.5
KC = D // P
FB = FF // P
CH = 512
TT = CH // P
CPB = L // CH
NCHUNK = B * CPB
G = B * H
NT = L // P
NQ = L // CH
MIX = D // DH
RING = 4
NBUF = 3
M_ROW = 3 * DH
POOL_TILES = [0, 1, 2, 3, 5, 6, 7, 9, 10, 11, 12]
PE_TILES = [t for t in range(NT) if t not in POOL_TILES]
NADD = len(POOL_TILES) - 1
HALVES = 2
FILLS = NQ * NT
FILLS_AT = (5, 5, 4, 4, 5, 4, 5, 4, 4, 5, 5, 4, 4, 4, 2, 0)
SPREAD = {0: (0, 0, 0, 0, 0), 2: (1, 1, 0, 0, 0), 4: (1, 1, 0, 1, 1), 5: (1, 1, 1, 1, 1)}
STEP_MAX = NT - 2
A_BANKS, B_BANKS = 3, 3
O_BANK, DEN_BANK = 6, 7
START = 1
STEPS_SPLIT, STEP_PROJECT, STEP_ROOT, STEP_TRANSPOSE = (2, 4), 6, 10, 15
AHEAD = 3
COL = P // 4
LOADS = 7


def block_kernel(nc, x, cT, wq, wk, wv, wo, w1, w2, wada, bqT, bkT, b1T, badaT, bada, bv, bo, b2, out):
    qk_hi = [nc.dram_tensor(f"{n}_hi", [B * D, L], F32, kind="Internal").ap() for n in "qk"]
    qk_lo = [nc.dram_tensor(f"{n}_lo", [B * D, L], F32, kind="Internal").ap() for n in "qk"]
    v_dram = nc.dram_tensor("v_rows", [L, B * D], F32, kind="Internal").ap()
    att_dram = nc.dram_tensor("attention_T", [D, B * L], F32, kind="Internal").ap()

    with ExitStack() as ctx:
        def sb(name, shape, dt=F32):
            return ctx.enter_context(nc.sbuf_tensor(name, shape, dt))

        def sem(name):
            return ctx.enter_context(nc.semaphore(name))

        weights_r = sb("weights_r", [P, 12288], F32R)
        w2_r = sb("w2_r", [P, 2, FB, D], F32R)
        acts_r = sb("acts_r", [P, 12288], F32R)
        work = sb("work", [P, 13824])
        ps = ctx.enter_context(nc.psum_tensor("ps", [P, 8, 512], F32))

        def view(t, at, *shape):
            n = 1
            for s in shape:
                n *= s
            ap = t[:, at:at + n]
            names = "abcd"[:len(shape)]
            if len(shape) == 1:
                return ap
            return ap.rearrange(f"p ({' '.join(names)}) -> p {' '.join(names)}",
                                **{k: s for k, s in zip(names[1:], shape[1:])})

        wqkv = view(weights_r, 0, 2, KC, 3 * D)
        wo_r = view(weights_r, 0, 2, KC, D)
        w1_r = view(weights_r, 2 * KC * D, 2, KC, FF)
        hT = [view(acts_r, (1 + p) * 2 * KC * CH, 2, KC, CH) for p in range(2)]
        qs = [view(acts_r, 4096 * u, L) for u in range(NBUF)]
        ks = [view(acts_r, 4096 * u + L, L) for u in range(NBUF)]
        oT_r = view(acts_r, 0, 2, KC, CH)
        g_r = view(acts_r, 4096, 4, 2, CH)
        h2T = view(acts_r, 8192, 2, KC, CH)
        assert [g % NBUF for g in range(G - 3, G)] == [2, 0, 1]

        x1c = [view(work, at, TT, D) for at in (0, 3584)]
        v_st = view(work, 2048, 2, D)
        hTf1 = view(work, 5632, KC, CH)
        stage = [view(work, 7680 + 2048 * i, KC, D) for i in range(2)]
        qk_st = view(work, 11776, 2, 2, CH)
        v_sb = [view(work, at, NT, DH) for at in (512, 0, 1024)]
        o_st = [view(work, at, CH) for at in (2560, 3072, 1536)]
        psum_acc = view(work, 3584, L)
        prob = view(work, 5632, RING, L)
        prob_slot = [view(work, 5632 + L * r, L) for r in range(RING)]
        SLOT_XC1, SLOT_XN3, SLOT_OTF, SLOT_HTF3 = range(RING)
        xc = [view(work, 512, TT, D), prob_slot[SLOT_XC1].rearrange("p (t d) -> p t d", d=D)]
        xn3 = prob_slot[SLOT_XN3].rearrange("p (t d) -> p t d", d=D)
        hTf3 = prob_slot[SLOT_HTF3].rearrange("p (k q) -> p k q", q=CH)
        oTf = prob_slot[SLOT_OTF].rearrange("p (k q) -> p k q", q=CH)
        gf = view(work, 3584, 2, CH)
        assert STEP_ROOT in POOL_TILES
        assert not any(NT - RING + s in POOL_TILES for s in (SLOT_XN3, SLOT_HTF3))

        tmp3 = sb("tmp3", [P, 2, D])
        gate = sb("gate", [P, 2, B, D])
        gate_b = sb("gate_b", [P, 2, B, D])
        bv_rows = sb("bv_rows", [P, D])
        mod = sb("mod", [P, 4, KC, B])
        ident = sb("ident", [P, P])
        ones = sb("ones", [P, P])
        recip = bv_rows
        c_sb = sb("c_sb", [P, KC, B])
        bq_sb = sb("bq_sb", [P, 2, KC])
        b1_sb = sb("b1_sb", [P, FB])
        bada_sb = sb("bada_sb", [P, 6, KC])
        stats = sb("stats", [P, TT, 6])
        mv = sb("mv", [P, TT, 2])
        var_eps = sb("var_eps", [P, TT])
        minus_half = sb("minus_half", [P, TT])
        rstd = sb("rstd", [P, TT])
        part_max = sb("part_max", [P, NT, NQ])
        row_max = sb("row_max", [P, NT])
        neg_max = sb("neg_max", [NT, P], F32R)
        mod_rows = tmp3[:, 0, :]
        cs_pad = tmp3[:, 1, 0:KC * COL].rearrange("p (k q) -> p k q", q=COL)
        sel_wide = tmp3[:, 1, P:P + B * P].rearrange("p (b q) -> p b q", q=P)
        sel = tmp3[:, 1, P + B * P:P + B * P + COL]

        consts_in = sem("consts_in")
        ada_in = [sem(f"ada_in{n}") for n in range(6)]
        w_in = [sem(f"w_in{n}") for n in range(5)]
        bv_in = sem("bv_in")
        bias_in = sem("bias_in")
        ident_ok = sem("ident_ok")
        ones_ok = sem("ones_ok")
        silu_ok = sem("silu_ok")
        pad_ok = sem("pad_ok")
        sel_ok = sem("sel_ok")
        ada_rows = sem("ada_rows")
        rows_ok = sem("rows_ok")
        ada_mm = sem("ada_mm")
        mod_ok = sem("mod_ok")
        gateb_ok = sem("gateb_ok")
        w_hi = sem("w_hi")
        w_lo = sem("w_lo")
        w2_lo = sem("w2_lo")
        late_in = [sem(f"late_in{i}") for i in range(2)]
        late_hi = sem("late_hi")
        late_lo = sem("late_lo")

        x_in = [sem(f"x_in{b}") for b in range(2)]
        stats_ok = sem("stats_ok")
        mv_ok = sem("mv_ok")
        eps_ok = sem("eps_ok")
        rstd_ok = sem("rstd_ok")
        xn_ok = sem("xn_ok")
        xT_mm = sem("xT_mm")
        hT_hi = sem("hT_hi")
        hT_lo = sem("hT_lo")
        qkv_mm = sem("qkv_mm")
        qk_hi_ok = sem("qk_hi_ok")
        qk_lo_ok = sem("qk_lo_ok")
        v_ok = sem("v_ok")
        qk_out = [sem(f"qk_out{s}") for s in range(2)]
        v_out = [sem(f"v_out{s}") for s in range(2)]

        ones_row = sem("ones_row")
        head_in = [sem(f"head_in{u}") for u in range(NBUF)]
        a_mm = sem("a_mm")
        a_max = sem("a_max")
        max_ok = sem("max_ok")
        maxT_mm = sem("maxT_mm")
        neg_ok = sem("neg_ok")
        neg_in = sem("neg_in")
        b_mm = sem("b_mm")
        exp_ok = sem("exp_ok")
        pv_mm = sem("pv_mm")
        add_ok = sem("add_ok")
        den_mm = sem("den_mm")
        o_raw = sem("o_raw")
        den_raw = sem("den_raw")
        rec_ok = sem("rec_ok")
        o_ok = sem("o_ok")
        o_out = [sem(f"o_out{u}") for u in range(NBUF)]

        xc_in = [sem(f"xc_in{b}") for b in range(2)]
        oT_in = sem("oT_in")
        oT_hi = sem("oT_hi")
        oT_lo = sem("oT_lo")
        o_mm = sem("o_mm")
        xg_ok = sem("xg_ok")
        o_tmp = sem("o_tmp")
        x1_ok = sem("x1_ok")
        stats3 = sem("stats3")
        mv3 = sem("mv3")
        eps3 = sem("eps3")
        rstd3 = sem("rstd3")
        xn3_ok = sem("xn3_ok")
        h2_mm = sem("h2_mm")
        h2_hi = sem("h2_hi")
        h2_lo = sem("h2_lo")
        m1_mm = sem("m1_mm")
        gelu_ok = sem("gelu_ok")
        g_hi = sem("g_hi")
        g_lo = sem("g_lo")
        m2_used = sem("m2_used")
        x1g_ok = sem("x1g_ok")
        m2_tmp = sem("m2_tmp")
        y_ok = sem("y_ok")
        y_out = [sem(f"y_out{b}") for b in range(2)]

        start_at_one = [pv_mm, add_ok, m1_mm, hT_lo, h2_lo, g_lo, m2_used, y_ok, hT_hi, h2_hi, v_ok, exp_ok, o_ok, gelu_ok, den_mm,
                        *v_out, *o_out]

        block = ctx.enter_context(nc.Block())

        def rows_of(w, c0):
            return w[:, c0:c0 + D].rearrange("(k p) n -> p k n", p=P)

        as_piece = lambda t: t[:].rearrange("p w b d -> p (w b) d")
        ADA = 6
        ada_at = [hTf1, as_piece(gate_b), stage[0], stage[1], stage[0], stage[1]]
        w_pieces = [(rows_of(w, 0), at, [wqkv[:, s, :, n * D:(n + 1) * D] for s in range(2)])
                    for n, (w, at) in enumerate(((wq, stage[0]), (wk, stage[1]), (wv, as_piece(gate))))]
        w_pieces += [(w2[n * D:(n + 1) * D, :].rearrange("(k p) n -> p k n", p=P), stage[n],
                      [w2_r[:, s, n * KC:(n + 1) * KC, :] for s in range(2)]) for n in range(2)]
        late = [(wo[k * P:(k + 1) * P, :], [wo_r[:, s, k, :] for s in range(2)]) for k in range(KC)]
        late += [(w1[k * P:(k + 1) * P, at:at + D], [w1_r[:, s, k, at:at + D] for s in range(2)])
                 for k in range(KC) for at in range(0, FF, D)]
        LATE_STEP = 2
        N_CONST = 5

        ORDER = [(0, 0), (0, 1), (1, 0), (0, 2), (1, 1), (0, 3), (1, 2), (1, 3)]
        assert NCHUNK == 8
        LOOP = 2
        T_AT = (0, 2, 4, 6)
        T_AT_0 = (5, 7, 9, 11)
        ADA_AT = {0: {7: 2, 10: 3}, 1: {5: 4, 10: 5}}
        W2_AT = {8: 3, 10: 4}
        BATCH0_DONE = 6
        FILLS_6 = {m: 3 for m in range(4, 12)}
        FILLS_7 = {m: 4 for m in range(10)}
        MAX_AT_7 = 10
        assert sum(FILLS_6.values()) + sum(FILLS_7.values()) == FILLS

        MM_CHUNK = 2 * KC + TT
        MOD_SHIFT1, MOD_SCALE1, MOD_SHIFT2, MOD_SCALE2 = range(4)
        MOD_OF = {0: MOD_SHIFT1, 1: MOD_SCALE1, 3: MOD_SHIFT2, 4: MOD_SCALE2}
        GATE_OF = {2: 0, 5: 1}

        @block.sync
        def _(sp):
            for s in start_at_one:
                sp.sem_inc(s, START)

            def load_x(b, c, dst, s):
                sp.dma_start(dst[b], x[b, bass.ds(c * CH, CH), :].rearrange("(t p) d -> p t d", p=P)).then_inc(s[b], 16)

            def load_x_mixed(p, b, c):
                rows = x[bass.ds(b, 1)].rearrange("o (p r) d -> p (o r) d", r=MIX)
                sp.dma_start(x1c[p], rows[:, bass.ds(c * TT, TT), :]).then_inc(x_in[p], 16)

            def load_ada(n):
                sp.dma_start(ada_at[n], rows_of(wada, n * D)).then_inc(ada_in[n], 16)

            def load_w(n):
                sp.dma_start(w_pieces[n][1], w_pieces[n][0]).then_inc(w_in[n], 16)

            def on_all_partitions(r):
                return r.rearrange("(o d) -> o d", o=1).broadcast_to((P, D))

            load_ada(0)
            load_x_mixed(0, *ORDER[0])
            load_ada(1)
            load_w(0)
            load_w(1)
            load_w(2)
            load_x_mixed(1, *ORDER[1])
            sp.dma_start(bv_rows[:], on_all_partitions(bv)).then_inc(bv_in, 16)
            sp.wait_ge(ada_mm, 2)
            for w, r in enumerate((bo, b2)):
                for b in range(B):
                    sp.dma_start(gate_b[:, w, b, :], on_all_partitions(r)).then_inc(bias_in, 16)
            for n in range(2):
                sp.wait_ge(w_hi, n + 1)
                sp.wait_ge(w_lo, n + 1)
                load_ada(2 + n)
            sp.wait_ge(w_hi, 3)
            sp.wait_ge(w_lo, 3)
            for w, r in enumerate((bada[2 * D:3 * D], bada[5 * D:6 * D])):
                for b in range(B):
                    sp.dma_start(gate[:, w, b, :], on_all_partitions(r)).then_inc(bias_in, 16)

            def store_qk(n, b, c, products=range(2 * KC)):
                for m in products:
                    t, blk = m // KC, m % KC
                    at = slice(b * D + blk * P, b * D + (blk + 1) * P)
                    sp.wait_ge(qk_lo_ok, n * 2 * KC + m + 1)
                    sp.dma_start(qk_hi[t][at, bass.ds(c * CH, CH)], qk_st[:, m % 2, 0, :]).then_inc(qk_out[m % 2], 16)
                    sp.dma_start(qk_lo[t][at, bass.ds(c * CH, CH)], qk_st[:, m % 2, 1, :]).then_inc(qk_out[m % 2], 16)

            def store_v(n, b, c, tiles=range(TT)):
                for t in tiles:
                    sp.wait_ge(v_ok, START + n * TT + t + 1)
                    sp.dma_start(v_dram[bass.ds(c * CH + t * P, P), b * D:(b + 1) * D], v_st[:, t % 2, :]).then_inc(v_out[t % 2], 16)

            def next_x(n, p, b, c):
                sp.wait_ge(xT_mm, (n + 1) * KC)
                load_x_mixed(p, b, c)

            def stored(chunks):
                for i in range(2):
                    sp.wait_ge(qk_out[i], 16 * 2 * KC * chunks)
                    sp.wait_ge(v_out[i], START + 16 * TT // 2 * chunks)

            for n in range(LOOP):
                next_x(n, n, *ORDER[n + 2])
                store_qk(n, *ORDER[n])
                if n == 0:
                    sp.wait_ge(ada_mm, 3)
                    load_ada(4)
                else:
                    sp.wait_ge(ada_mm, 5)
                    load_w(3)
                store_v(n, *ORDER[n])
                if n == 0:
                    sp.wait_ge(ada_mm, 4)
                    load_ada(5)
                else:
                    sp.wait_ge(ada_mm, 6)
                    load_w(4)
            with sp.Fori(0, 2) as i:
                n = i * 2 + LOOP
                next_x(n, 0, 1, i + 1)
                store_qk(n, 1, i)
                store_v(n, 1, i)
                n = i * 2 + LOOP + 1
                next_x(n, 1, i, CPB - 1)
                store_qk(n, 0, i + 2)
                store_v(n, 0, i + 2)

            def load_head(g, u):
                r = bass.ds(g * DH, DH)
                for blk, (q, k) in enumerate(((qk_hi, qk_hi), (qk_hi, qk_lo), (qk_lo, qk_hi))):
                    at = slice(blk * DH, (blk + 1) * DH)
                    sp.dma_start(qs[u][at, :].bitcast(F32), q[0][r, :]).then_inc(head_in[u], 16)
                    sp.dma_start(ks[u][at, :].bitcast(F32), k[1][r, :]).then_inc(head_in[u], 16)
                sp.dma_start(v_sb[u], v_dram[:, r].rearrange("(t p) d -> p t d", p=P)).then_inc(head_in[u], 16)

            def put_max(g, u):
                sp.wait_ge(neg_ok, g + 1)
                sp.dma_start(qs[u][M_ROW:M_ROW + 1, :].bitcast(F32),
                             neg_max[:].bitcast(F32)).then_inc(neg_in, 16)

            def store_head(g, u):
                sp.wait_ge(o_ok, START + g + 1)
                for j in range(NQ):
                    sp.dma_start(att_dram[j * P:(j + 1) * P, bass.ds(g * P, P)].rearrange("(r d) q -> d r q", d=DH),
                                 o_st[u][j * DH:(j + 1) * DH, :].rearrange("d (r q) -> d r q", q=P)).then_inc(o_out[u], 16)

            def stage2(g, u, load):
                if load:
                    sp.wait_ge(den_mm, START + g)
                    load_head(g + 2, (u + 2) % NBUF)
                put_max(g + 1, (u + 1) % NBUF)
                store_head(g - 1, (u + 2) % NBUF)

            store_qk(NCHUNK - 2, *ORDER[NCHUNK - 2], range(2))
            stored(BATCH0_DONE)
            sp.wait_ge(xT_mm, (NCHUNK - 1) * KC)
            load_head(0, 0)
            store_qk(NCHUNK - 2, *ORDER[NCHUNK - 2], range(2, 2 * KC))
            store_v(NCHUNK - 2, *ORDER[NCHUNK - 2])
            sp.wait_ge(qkv_mm, (NCHUNK - 1) * MM_CHUNK)
            load_head(1, 1)
            store_qk(NCHUNK - 1, *ORDER[NCHUNK - 1])
            store_v(NCHUNK - 1, *ORDER[NCHUNK - 1], range(2))
            put_max(0, 0)
            store_v(NCHUNK - 1, *ORDER[NCHUNK - 1], range(2, TT))
            for k, (rows, _) in enumerate(late):
                if k == 0:
                    sp.wait_ge(ada_mm, ADA)
                if k >= 2:
                    sp.wait_ge(late_hi, k - 1)
                    sp.wait_ge(late_lo, k - 1)
                sp.dma_start(tmp3[:, k % 2, :], rows).then_inc(late_in[k % 2], 16)
                if k == 1:
                    sp.wait_ge(qkv_mm, NCHUNK * MM_CHUNK)
                    stored(NCHUNK)
                    load_head(2, 2)
            put_max(1, 1)
            with sp.Fori(0, G // NBUF - 1) as i:
                for k in range(1, NBUF + 1):
                    stage2(i * NBUF + k, k % NBUF, True)
            def heads_stored(n):
                for u in range(NBUF):
                    sp.wait_ge(o_out[u], START + 16 * NQ * len(range(u, n, NBUF)))

            def rows_oT(b, c):
                return att_dram[:, bass.ds(b * L + c * CH, CH)].rearrange("(k p) q -> p k q", p=P)

            def load_oT(b, c):
                sp.dma_start(oTf, rows_oT(b, c)).then_inc(oT_in, 16)

            def load_first_oT(half):
                if half:
                    sp.wait_ge(oT_hi, 2)
                    sp.wait_ge(oT_lo, 2)
                sp.dma_start(tmp3[:], rows_oT(0, 0)[:, 2 * half:2 * half + 2, :]).then_inc(oT_in, 16)

            for g in range(G // NBUF * NBUF - NBUF + 1, G - 1):
                stage2(g, g % NBUF, g + 2 < G)
            load_first_oT(0)
            heads_stored(G - 2)
            sp.wait_ge(den_mm, START + G - 1)
            load_x(0, 0, xc, xc_in)
            store_head(G - 2, (G - 2) % NBUF)
            load_first_oT(1)
            sp.wait_ge(pv_mm, START + G * NT)
            sp.wait_ge(add_ok, START + G * (NADD * HALVES))
            load_oT(1, 0)
            load_x(1, 0, xc, xc_in)
            store_head(G - 1, (G - 1) % NBUF)
            heads_stored(G)

            def stage3(c, b, more):
                n = c * 2 + b
                if more:
                    sp.wait_ge(oT_hi, (n + 2) * KC)
                    sp.wait_ge(oT_lo, (n + 2) * KC)
                    load_oT(b, c + 1)
                sp.wait_ge(y_ok, START + (n + 1) * TT)
                sp.dma_start(out[b, bass.ds(c * CH, CH), :].rearrange("(t p) d -> p t d", p=P), xc[b]).then_inc(y_out[b], 16)
                if more:
                    sp.wait_ge(y_out[b], c * 16 + 16)
                    load_x(b, c + 1, xc, xc_in)

            with sp.Fori(0, CPB - 1) as c:
                for b in range(2):
                    stage3(c, b, True)
            stage3(CPB - 1, 0, False)
            for t in range(TT):
                sp.wait_ge(y_ok, START + (NCHUNK - 1) * TT + t + 1)
                sp.dma_start(out[1, (CPB - 1) * CH + t * P:(CPB - 1) * CH + (t + 1) * P, :], xc[1][:, t, :]).then_inc(y_out[1], 16)
            sp.wait_ge(y_out[0], 16 * CPB)
            sp.wait_ge(y_out[1], 16 * (CPB - 1 + TT))

        @block.gpsimd
        def _(pool):
            nc.gpsimd.memset(ident[:], 0.0).then_inc(ident_ok, 1)
            pool.wait_ge(ident_ok, 1)
            nc.gpsimd.affine_select(out=ident[:], in_=ident[:], compare_op=ALU.not_equal, fill=1.0, base=0,
                                    pattern=[[-1, P]], channel_multiplier=1).then_inc(ident_ok, 1)
            nc.gpsimd.memset(minus_half[:], -0.5).then_inc(ident_ok, 1)
            pool.wait_ge(ident_ok, 3)

            def root(n, wait, added, done):
                pool.wait_ge(wait, (n + 1) * TT)
                nc.gpsimd.tensor_tensor(var_eps[:], var_eps[:], mv[:, :, 1], ALU.add).then_inc(added, 1)
                pool.wait_ge(added, n + 1)
                nc.gpsimd.tensor_tensor(rstd[:], var_eps[:], minus_half[:], ALU.pow).then_inc(done, 1)

            def row_of_ones(u):
                nc.gpsimd.memset(ks[u][M_ROW:M_ROW + 1, :].bitcast(F32), 1.0).then_inc(ones_row, 1)
                pool.wait_ge(ones_row, u + 1)

            row_of_ones(0)
            with pool.Fori(0, NCHUNK) as n:
                root(n, mv_ok, eps_ok, rstd_ok)
            for n in (3, 4):
                _, src, (hi, lo) = w_pieces[n]
                pool.wait_ge(w_hi, n + 1)
                nc.gpsimd.tensor_tensor(lo, src, hi.bitcast(F32), ALU.subtract).then_inc(w2_lo, 1)
            pool.wait_ge(w2_lo, 2)
            pool.wait_ge(qkv_mm, NCHUNK * MM_CHUNK)
            for u in range(1, NBUF):
                row_of_ones(u)

            def sum_probs(g, between={}):
                pool.wait_ge(den_mm, START + g)
                for k in range(NADD):
                    t = POOL_TILES[k + 1]
                    if t in between:
                        between[t]()
                    for h in range(HALVES):
                        pool.wait_ge(exp_ok, START + g * (NT * NQ) + t * NQ + (h + 1) * NQ // HALVES)
                        at = slice(h * L // HALVES, (h + 1) * L // HALVES)
                        if k:
                            pool.wait_ge(add_ok, START + (g * NADD + k - 1) * HALVES + h + 1)
                        first = prob[:, POOL_TILES[0] % RING, at] if k == 0 else psum_acc[:, at]
                        nc.gpsimd.tensor_tensor(psum_acc[:, at], first, prob[:, t % RING, at], ALU.add).then_inc(add_ok, 1)

            with pool.Fori(0, G - 1) as g:
                sum_probs(g)
            sum_probs(G - 1, {STEP_ROOT: lambda: root(0, mv3, eps3, rstd3)})

            def add_bias(n, b, which, done):
                for t in range(TT):
                    nc.gpsimd.tensor_tensor(xc[b][:, t, :], xc[b][:, t, :], gate_b[:, which, b, :], ALU.add).then_inc(done, 1)

            def stage3(c, b, nxt):
                n = c * 2 + b
                pool.wait_ge(xn3_ok, (n + 1) * TT)
                add_bias(n, b, 1, x1g_ok)
                if nxt:
                    pool.wait_ge(xc_in[1 - b], (c + b) * 16 + 16)
                    add_bias(n + 1, 1 - b, 0, xg_ok)
                    root(n + 1, mv3, eps3, rstd3)

            with pool.Fori(0, CPB - 1) as c:
                for b in range(2):
                    stage3(c, b, True)
            stage3(CPB - 1, 0, True)
            stage3(CPB - 1, 1, False)

        @block.scalar
        def _(act):
            consts = ((c_sb[:], cT), (bada_sb[:], badaT), (bq_sb[:, 0, :], bqT), (bq_sb[:, 1, :], bkT), (b1_sb[:], b1T))
            for dst, src in consts:
                act.dma_start(dst, src).then_inc(consts_in, 16)
            assert len(consts) == N_CONST
            act.wait_ge(consts_in, 16 * N_CONST)
            act.wait_ge(pad_ok, 1)
            nc.scalar.activation(cs_pad[:, :, 0:B], c_sb[:], ACT.Silu).then_inc(silu_ok, 1)

            def take_rows(n):
                act.wait_ge(ada_rows, n + 1)
                if n:
                    act.wait_ge(ada_mm, n)
                nc.scalar.activation(mod_rows, ps[:, 7, :], ACT.Copy).then_inc(rows_ok, 1)

            def split_hi(n):
                act.wait_ge(w_in[n], 16)
                nc.scalar.activation(w_pieces[n][2][0], w_pieces[n][1], ACT.Copy).then_inc(w_hi, 1)

            def modulate(n, b, blk, wait, used, hTf, h, shift, scale, done):
                act.wait_ge(wait, n * KC + blk + 1)
                act.wait_ge(used, START + n * KC)
                kw = dict(scale=mod[:, scale, blk, b:b + 1], bias=mod[:, shift, blk, b:b + 1])
                nc.scalar.activation(h[:, 0, blk, :], ps[:, blk % 2, :], ACT.Identity, **kw)
                nc.scalar.activation(hTf[:, blk, :], ps[:, blk % 2, :], ACT.Identity, **kw).then_inc(done, 1)

            def modulate1(n, p, b, blk):
                if not (isinstance(n, int) and n < 2):
                    act.wait_ge(qkv_mm, (n - 1) * MM_CHUNK)
                modulate(n, b, blk, xT_mm, hT_lo, hTf1, hT[p], MOD_SHIFT1, MOD_SCALE1, hT_hi)

            def chunk(n, p, b_next, at=T_AT, ada={}, w2_at={}):
                for m in range(MM_CHUNK):
                    if m < 2 * KC:
                        act.wait_ge(qkv_mm, n * MM_CHUNK + m + 1)
                        if not (isinstance(n, int) and n == 0 and m < 2):
                            act.wait_ge(qk_out[m % 2], (n * KC + m // 2) * 32)
                        nc.scalar.activation(qk_st[:, m % 2, 0, :].bitcast(F32R), ps[:, 2 + m % 4, :], ACT.Identity,
                                             bias=bq_sb[:, m // KC, m % KC:m % KC + 1]).then_inc(qk_hi_ok, 1)
                    if b_next is not None and m in at:
                        modulate1(n + 1, 1 - p, b_next, at.index(m))
                    if m in ada:
                        take_rows(ada[m])
                    if m in w2_at:
                        split_hi(w2_at[m])

            take_rows(0)
            split_hi(0)
            take_rows(1)
            split_hi(1)
            act.wait_ge(mod_ok, 2)
            for blk in range(KC):
                modulate1(0, 0, ORDER[0][0], blk)
            split_hi(2)
            chunk(0, 0, ORDER[1][0], T_AT_0, ADA_AT[0])
            chunk(1, 1, ORDER[2][0], ada=ADA_AT[1])
            with act.Fori(0, 2) as i:
                chunk(i * 2 + LOOP, 0, 0)
                chunk(i * 2 + LOOP + 1, 1, 1)
            chunk(NCHUNK - 2, 0, ORDER[NCHUNK - 1][0], w2_at=W2_AT)
            chunk(NCHUNK - 1, 1, None)
            act.wait_ge(hT_lo, START + NCHUNK * KC)
            act.wait_ge(w2_lo, 2)
            for i in range(2):
                act.wait_ge(qk_out[i], 16 * 2 * KC * NCHUNK)

            def split_late_hi(k):
                act.wait_ge(late_in[k % 2], 16 * (k // 2 + 1))
                nc.scalar.activation(late[k][1][0], tmp3[:, k % 2, :], ACT.Copy).then_inc(late_hi, 1)

            def take_output(g, u, uses):
                act.wait_ge(pv_mm, START + (g + 1) * NT)
                act.wait_ge(o_out[u], START + uses * (16 * NQ))
                nc.scalar.activation(o_st[u], ps[:, O_BANK, :], ACT.Copy).then_inc(o_raw, 1)

            def take_denominator(g):
                act.wait_ge(den_mm, START + g + 1)
                act.wait_ge(o_ok, START + g)
                nc.scalar.activation(recip[:], ps[:, DEN_BANK, :], ACT.Copy).then_inc(den_raw, 1)

            def split_oT(n):
                act.wait_ge(oT_in, n * 16 + 32)
                act.wait_ge(o_mm, n * TT)
                for blk in range(KC):
                    nc.scalar.activation(oT_r[:, 0, blk, :], oTf[:, blk, :], ACT.Copy).then_inc(oT_hi, 1)

            def probs(g, u, uses, prev, between={}):
                for t in range(NT):
                    last, gl = ((t - RING) % NT, g if t >= RING else g - 1)
                    if t >= RING or prev:
                        act.wait_ge(pv_mm, START + gl * NT + last + 1)
                        if last in POOL_TILES:
                            act.wait_ge(add_ok, START + gl * (NADD * HALVES) + max(POOL_TILES.index(last), 1) * HALVES)
                    for j in range(NQ):
                        act.wait_ge(b_mm, g * (NT * NQ) + t * NQ + j + 1)
                        nc.scalar.activation(prob[:, t % RING, j * CH:(j + 1) * CH], ps[:, A_BANKS + (u + t * NQ + j) % B_BANKS, :],
                                             ACT.Exp, scale=SCALE).then_inc(exp_ok, 1)
                    if prev and t == 0:
                        take_output(g - 1, (u + 2) % NBUF, uses)
                    if prev and t == 1:
                        take_denominator(g - 1)
                    if t in between:
                        between[t]()

            probs(0, 0, 0, False, {LATE_STEP + k: lambda k=k: split_late_hi(k) for k in range(len(late))})
            for i in range(2):
                act.wait_ge(v_out[i], START + 16 * NCHUNK * TT // 2)
            with act.Fori(0, G // NBUF) as i:
                for k in range(1, NBUF + 1):
                    probs(i * NBUF + k, k % NBUF, i, True)
            def split_first_oT(half):
                act.wait_ge(oT_in, 16 * half + 16)
                for k in range(2):
                    nc.scalar.activation(oT_r[:, 0, 2 * half + k, :], tmp3[:, k, :], ACT.Copy).then_inc(oT_hi, 1)

            probs(G - 1, (G - 1) % NBUF, (G - 2) // NBUF, True, {t: lambda h=h: split_first_oT(h) for h, t in enumerate(STEPS_SPLIT)})

            def modulate3(n, b):
                act.wait_ge(m1_mm, START + n * FB)
                for blk in range(KC):
                    modulate(n, b, blk, h2_mm, h2_lo, hTf3, h2T, MOD_SHIFT2, MOD_SCALE2, h2_hi)

            act.wait_ge(pv_mm, START + (G - 1) * NT + NT - RING + SLOT_HTF3 + 1)
            modulate3(0, 0)
            take_output(G - 1, (G - 1) % NBUF, (G - 1) // NBUF)
            take_denominator(G - 1)

            def stage3(c, b, nxt):
                n = c * 2 + b
                for f in range(FB):
                    if nxt and f == 2:
                        split_oT(n + 1)
                    act.wait_ge(m1_mm, START + n * FB + f + 1)
                    if f >= 2:
                        act.wait_ge(g_lo, START + n * FB + f - 1)
                    else:
                        act.wait_ge(g_lo, START + n * FB)
                    nc.scalar.activation(gf[:, f % 2, :], ps[:, 2 + f % 2, :], ACT.Gelu, bias=b1_sb[:, f:f + 1]).then_inc(gelu_ok, 1)
                if nxt:
                    modulate3(n + 1, 1 - b)

            with act.Fori(0, CPB - 1) as c:
                for b in range(2):
                    stage3(c, b, True)
            stage3(CPB - 1, 0, True)
            stage3(CPB - 1, 1, False)

        @block.vector
        def _(dve):
            nc.vector.memset(cs_pad, 0.0).then_inc(pad_ok, 1)
            nc.vector.memset(ones[:], 1.0).then_inc(ones_ok, 1)
            dve.wait_ge(ident_ok, 3)
            nc.vector.tensor_reduce(sel, ident[:].rearrange("p (k q) -> p q k", q=COL), AX.X, ALU.add).then_inc(sel_ok, 1)
            dve.wait_ge(ones_ok, 1)
            dve.wait_ge(sel_ok, 1)
            for b in range(B):
                nc.vector.tensor_scalar(sel_wide[:, b, :], ones[:], sel[:, b:b + 1], None, ALU.mult).then_inc(sel_ok, 1)
            def split_lo(n):
                dve.wait_ge(w_hi, n + 1)
                _, src, (hi, lo) = w_pieces[n]
                nc.vector.tensor_tensor(lo, src, hi.bitcast(F32), ALU.subtract).then_inc(w_lo, 1)

            def take_ada(n):
                dve.wait_ge(ada_mm, n + 1)
                if n in MOD_OF:
                    dve.wait_ge(consts_in, 16 * N_CONST)
                    for b in range(B):
                        ins = nc.vector.scalar_tensor_tensor(
                            out=mod[:, MOD_OF[n], :, b], in0=ps[:, 6, 0:KC * B].rearrange("p (k b) -> p k b", b=B)[:, :, b],
                            scalar=1.0 if n in (1, 4) else 0.0, in1=bada_sb[:, n, :], op0=ALU.add, op1=ALU.add)
                    ins.then_inc(mod_ok, 1)
                else:
                    w = GATE_OF[n]
                    dve.wait_ge(bias_in, 16 * 4 * B)
                    for b in range(B):
                        ins = nc.vector.tensor_tensor(gate[:, w, b, :], ps[:, 6 + b, :], gate[:, w, b, :], ALU.add)
                    ins.then_inc(mod_ok, 1)
                    dve.wait_ge(mod_ok, n + 1)
                    for b in range(B):
                        nc.vector.tensor_tensor(gate_b[:, w, b, :], gate_b[:, w, b, :], gate[:, w, b, :], ALU.mult).then_inc(gateb_ok, 1)

            def norm_stats(n, src, ok, tiles=range(TT)):
                for t in tiles:
                    nc.vector.bn_stats(stats[:, t, :], src[:, t, :]).then_inc(ok, 1)

            def norm_mean(n, ok, done):
                dve.wait_ge(ok, (n + 1) * TT)
                nc.vector.memset(var_eps[:], EPS)
                for t in range(TT):
                    nc.vector.bn_aggr(mv[:, t, :], stats[:, t, :]).then_inc(done, 1)

            def norm_apply(n, src, dst, ok, done):
                dve.wait_ge(ok, n + 1)
                for t in range(TT):
                    nc.vector.tensor_scalar(dst[:, t, :], src[:, t, :], mv[:, t, 0:1], rstd[:, t:t + 1],
                                            ALU.subtract, ALU.mult).then_inc(done, 1)

            def x_stats(n, p, turn, tiles):
                dve.wait_ge(x_in[p], turn * 16 + 16)
                if not (isinstance(n, int) and n == 0):
                    dve.wait_ge(xn_ok, n * TT)
                norm_stats(n, x1c[p], stats_ok, tiles)

            def norm1(n, p):
                x_stats(n, p, 0, range(TT))
                norm_mean(n, stats_ok, mv_ok)
                norm_apply(n, x1c[p], x1c[p], rstd_ok, xn_ok)

            def remainder(n, blk, hi_ok, hTf, h, done):
                dve.wait_ge(hi_ok, START + n * KC + blk + 1)
                nc.vector.tensor_tensor(h[:, 1, blk, :], hTf[:, blk, :], h[:, 0, blk, :].bitcast(F32), ALU.subtract).then_inc(done, 1)

            def take(n, m):
                if m < 2 * KC:
                    dve.wait_ge(qk_hi_ok, n * 2 * KC + m + 1)
                    nc.vector.scalar_tensor_tensor(
                        out=qk_st[:, m % 2, 1, :].bitcast(F32R), in0=ps[:, 2 + m % 4, :], scalar=bq_sb[:, m // KC, m % KC:m % KC + 1],
                        in1=qk_st[:, m % 2, 0, :], op0=ALU.add, op1=ALU.subtract).then_inc(qk_lo_ok, 1)
                else:
                    t = m - 2 * KC
                    dve.wait_ge(qkv_mm, n * MM_CHUNK + m + 1)
                    dve.wait_ge(v_out[t % 2], START + (n * (TT // 2) + t // 2) * 16)
                    nc.vector.tensor_tensor(v_st[:, t % 2, :], ps[:, 2 + t % 4, :], bv_rows[:], ALU.add).then_inc(v_ok, 1)

            def first_max(f):
                dve.wait_ge(a_mm, f + 1)
                nc.vector.tensor_reduce(part_max[:, f // NQ, f % NQ:f % NQ + 1], ps[:, 6 + f % 2, :], AX.X, ALU.max).then_inc(a_max, 1)

            def row_maxima(g):
                dve.wait_ge(a_max, (g + 1) * FILLS)
                nc.vector.tensor_reduce(row_max[:], part_max[:], AX.X, ALU.max).then_inc(max_ok, 1)

            def negate_max(g):
                dve.wait_ge(maxT_mm, g + 1)
                if not isinstance(g, int) or g:
                    dve.wait_ge(neg_in, g * 16)
                nc.vector.tensor_scalar(neg_max[:], ps[0:NT, 0, 0:P], -1.0, None, ALU.mult).then_inc(neg_ok, 1)

            fills = iter(range(FILLS))

            def chunk(n, p, turn, nxt=True, nxt2=True, at=T_AT, ada={}, max_after={}, max_at=None):
                for m in range(MM_CHUNK):
                    for _ in range(max_after.get(m, 0)):
                        first_max(next(fills))
                    if m == max_at:
                        row_maxima(0)
                    take(n, m)
                    if m == max_at:
                        negate_max(0)
                    if nxt and m in at:
                        remainder(n + 1, at.index(m), hT_hi, hTf1, hT[1 - p], hT_lo)
                    if m - 1 in ada:
                        take_ada(ada[m - 1])
                    if nxt2 and m in (1, 3, 5, 7):
                        x_stats(n + 2, p, turn + 1, [m // 2])
                    if nxt2 and m == 8:
                        norm_mean(n + 2, stats_ok, mv_ok)
                    if nxt2 and m == 10:
                        norm_apply(n + 2, x1c[p], x1c[p], rstd_ok, xn_ok)

            norm1(0, 0)
            take_ada(0)
            split_lo(0)
            take_ada(1)
            split_lo(1)
            for blk in range(KC):
                remainder(0, blk, hT_hi, hTf1, hT[0], hT_lo)
            split_lo(2)
            norm1(1, 1)
            dve.wait_ge(bv_in, 16)
            chunk(0, 0, 0, at=T_AT_0, ada=ADA_AT[0])
            chunk(1, 1, 0, ada=ADA_AT[1])
            with dve.Fori(0, 2) as i:
                for p in range(2):
                    chunk(i * 2 + LOOP + p, p, i + 1)
            chunk(NCHUNK - 2, 0, CPB - 1, nxt2=False, max_after=FILLS_6)
            chunk(NCHUNK - 1, 1, CPB - 1, nxt=False, nxt2=False, max_after=FILLS_7, max_at=MAX_AT_7)
            assert next(fills, None) is None

            def find_max(g, u, between={}):
                for f in range(FILLS):
                    if f in between:
                        between[f]()
                    dve.wait_ge(a_mm, g * FILLS + f + 1)
                    nc.vector.tensor_reduce(part_max[:, f // NQ, f % NQ:f % NQ + 1], ps[:, (u + f) % A_BANKS, :], AX.X, ALU.max).then_inc(a_max, 1)
                row_maxima(g)
                negate_max(g)

            def normalise(g, u):
                dve.wait_ge(den_raw, g + 1)
                nc.vector.reciprocal(recip[:], recip[:]).then_inc(rec_ok, 1)
                dve.wait_ge(o_raw, g + 1)
                dve.wait_ge(rec_ok, g + 1)
                nc.vector.tensor_tensor(o_st[u], o_st[u], recip[:], ALU.mult).then_inc(o_ok, 1)

            def split_late_lo(k):
                dve.wait_ge(late_hi, k + 1)
                hi, lo = late[k][1]
                nc.vector.tensor_tensor(lo, tmp3[:, k % 2, :], hi.bitcast(F32), ALU.subtract).then_inc(late_lo, 1)

            find_max(1, 1, {4 * (LATE_STEP + 2 + k) + 2: lambda k=k: split_late_lo(k) for k in range(len(late))})
            with dve.Fori(0, G // NBUF) as i:
                for k in range(1, NBUF + 1):
                    find_max(i * NBUF + k + 1, (k + 1) % NBUF)
                    normalise(i * NBUF + k - 1, (k - 1) % NBUF)
            normalise(G - 2, (G - 2) % NBUF)

            def oT_rest(n):
                for blk in range(KC):
                    dve.wait_ge(oT_hi, n * KC + blk + 1)
                    whole = tmp3[:, blk % 2, :] if isinstance(n, int) and n == 0 else oTf[:, blk, :]
                    nc.vector.tensor_tensor(oT_r[:, 1, blk, :], whole, oT_r[:, 0, blk, :].bitcast(F32), ALU.subtract).then_inc(oT_lo, 1)

            def residual1(n, b):
                for t in range(TT):
                    dve.wait_ge(o_mm, n * TT + t + 1)
                    if t >= 2:
                        dve.wait_ge(x1_ok, n * TT + t - 1)
                    elif not isinstance(n, int) or n:
                        dve.wait_ge(y_ok, START + (n - 1) * TT)
                    nc.vector.tensor_tensor(tmp3[:, t % 2, :], ps[:, t % 2, :], gate[:, 0, b, :], ALU.mult).then_inc(o_tmp, 1)
                    dve.wait_ge(xg_ok, n * TT + t + 1)
                    dve.wait_ge(o_tmp, n * TT + t + 1)
                    nc.vector.tensor_tensor(xc[b][:, t, :], xc[b][:, t, :], tmp3[:, t % 2, :], ALU.add).then_inc(x1_ok, 1)

            def stats_of(n, b):
                dve.wait_ge(x1_ok, (n + 1) * TT)
                norm_stats(n, xc[b], stats3)

            def split_gelu(n, f):
                dve.wait_ge(gelu_ok, START + n * FB + f + 1)
                if f >= 4:
                    dve.wait_ge(m2_used, START + n * FB + f - 3)
                else:
                    dve.wait_ge(m2_used, START + n * FB)
                nc.vector.tensor_copy(g_r[:, f % 4, 0, :], gf[:, f % 2, :]).then_inc(g_hi, 1)
                dve.wait_ge(g_hi, n * FB + f + 1)
                nc.vector.tensor_tensor(g_r[:, f % 4, 1, :], gf[:, f % 2, :], g_r[:, f % 4, 0, :].bitcast(F32), ALU.subtract).then_inc(g_lo, 1)

            def residual2(n, b):
                dve.wait_ge(m2_used, START + (n + 1) * FB)
                for t in range(TT):
                    if t >= 2:
                        dve.wait_ge(y_ok, START + n * TT + t - 1)
                    else:
                        dve.wait_ge(y_ok, START + n * TT)
                    nc.vector.tensor_tensor(tmp3[:, t % 2, :], ps[:, 4 + t, :], gate[:, 1, b, :], ALU.mult).then_inc(m2_tmp, 1)
                    dve.wait_ge(m2_tmp, n * TT + t + 1)
                    dve.wait_ge(x1g_ok, n * TT + t + 1)
                    nc.vector.tensor_tensor(xc[b][:, t, :], xc[b][:, t, :], tmp3[:, t % 2, :], ALU.add).then_inc(y_ok, 1)

            dve.wait_ge(xc_in[0], 16)
            for t in range(TT):
                nc.vector.tensor_tensor(xc[0][:, t, :], xc[0][:, t, :], gate_b[:, 0, 0, :], ALU.add).then_inc(xg_ok, 1)
            oT_rest(0)
            residual1(0, 0)
            stats_of(0, 0)
            norm_mean(0, stats3, mv3)
            dve.wait_ge(pv_mm, START + (G - 1) * NT + NT - RING + SLOT_XN3 + 1)
            norm_apply(0, xc[0], xn3, rstd3, xn3_ok)
            for blk in range(KC):
                remainder(0, blk, h2_hi, hTf3, h2T, h2_lo)
            normalise(G - 1, (G - 1) % NBUF)

            def stage3(c, b, nxt):
                n = c * 2 + b
                split_gelu(n, 0)
                split_gelu(n, 1)
                if nxt:
                    oT_rest(n + 1)
                split_gelu(n, 2)
                split_gelu(n, 3)
                if nxt:
                    residual1(n + 1, 1 - b)
                    stats_of(n + 1, 1 - b)
                split_gelu(n, 4)
                if nxt:
                    norm_mean(n + 1, stats3, mv3)
                split_gelu(n, 5)
                if nxt:
                    norm_apply(n + 1, xc[1 - b], xn3, rstd3, xn3_ok)
                split_gelu(n, 6)
                split_gelu(n, 7)
                if nxt:
                    for blk in range(KC):
                        remainder(n + 1, blk, h2_hi, hTf3, h2T, h2_lo)
                residual2(n, b)

            with dve.Fori(0, CPB - 1) as c:
                for b in range(2):
                    stage3(c, b, True)
            stage3(CPB - 1, 0, True)
            stage3(CPB - 1, 1, False)

        @block.tensor
        def _(pe):
            def multiply_piece(n):
                pe.wait_ge(ada_in[n], 16)
                pe.wait_ge(silu_ok, 1)
                if n:
                    pe.wait_ge(rows_ok, n)
                    pe.wait_ge(mod_ok, n)
                for kk in range(KC):
                    mm = nc.tensor.matmul(ps[kk * COL:(kk + 1) * COL, 7, :], cs_pad[:, kk, :], ada_at[n][:, kk, :], start=True, stop=True)
                mm.then_inc(ada_rows, 1)

            def spread_rows(n):
                pe.wait_ge(rows_ok, n + 1)
                pe.wait_ge(sel_ok, 1 + B)
                if n in MOD_OF:
                    for blk in range(KC):
                        mm = nc.tensor.matmul(ps[:, 6, blk * B:(blk + 1) * B], mod_rows[:, blk * P:(blk + 1) * P], sel[:, 0:B], start=True, stop=True)
                else:
                    for b in range(B):
                        mm = nc.tensor.matmul(ps[:, 6 + b, :], sel_wide[:, b, :], mod_rows, start=True, stop=True)
                mm.then_inc(ada_mm, 1)

            def product(o, lhs, rhs, between=lambda: None):
                for kk in range(KC):
                    if kk:
                        between()
                    for s, r in ((0, 0), (0, 1), (1, 0)):
                        mm = nc.tensor.matmul(o, lhs(s, kk), rhs(r, kk), start=(kk == 0 and s == r), stop=(kk == KC - 1 and s == 1))
                return mm

            def transposes(n, src, wait, used, done, blocks=range(KC)):
                pe.wait_ge(wait, (n + 1) * TT)
                for blk in blocks:
                    pe.wait_ge(used, START + n * KC + max(blk - 1, 0))
                    for t in range(TT):
                        mm = nc.tensor.transpose(ps[:, blk % 2, t * P:(t + 1) * P], src[:, t, blk * P:(blk + 1) * P], ident[:])
                    mm.then_inc(done, 1)

            def qkv(n, p, m, between):
                h = hT[p]
                if m == 0:
                    pe.wait_ge(hT_lo, START + (n + 1) * KC)
                if m >= 4:
                    pe.wait_ge(qk_lo_ok, n * 2 * KC + m - 3)
                elif not (isinstance(n, int) and n == 0):
                    pe.wait_ge(v_ok, START + (n - 1) * TT + m + 1)
                if m < 2 * KC:
                    mm = product(ps[:, 2 + m % 4, :], lambda s, kk: wqkv[:, s, kk, m * P:(m + 1) * P], lambda s, kk: h[:, s, kk, :], between)
                else:
                    t = m - 2 * KC
                    mm = product(ps[:, 2 + m % 4, :], lambda s, kk: h[:, s, kk, t * P:(t + 1) * P],
                                 lambda s, kk: wqkv[:, s, kk, 2 * D:3 * D], between)
                mm.then_inc(qkv_mm, 1)

            def transpose_max(g):
                pe.wait_ge(max_ok, g + 1)
                nc.tensor.matmul(ps[0:NT, 0, 0:P], row_max[:], ident[:], start=True, stop=True).then_inc(maxT_mm, 1)

            fills = iter(range(FILLS))

            def first_max_scores():
                f = next(fills)
                if f == 0:
                    pe.wait_ge(head_in[0], 16 * LOADS)
                if f >= 2:
                    pe.wait_ge(a_max, f - 1)
                j = f % NQ
                nc.tensor.matmul(ps[:, 6 + f % 2, :], qs[0][0:M_ROW, f // NQ * P:(f // NQ + 1) * P],
                                 ks[0][0:M_ROW, j * CH:(j + 1) * CH], start=True, stop=True).then_inc(a_mm, 1)

            def chunk(n, p, nxt=True, at=T_AT, ada={}, max_after={}, max_at=None):
                for m in range(MM_CHUNK):
                    left = [max_after.get(m, 0)]

                    def between():
                        if left[0]:
                            left[0] -= 1
                            first_max_scores()

                    if isinstance(n, int) and n == 0 and m % KC == 0:
                        pe.wait_ge(w_lo, m // KC + 1)
                    qkv(n, p, m, between)
                    between()
                    assert not left[0]
                    if nxt and m in at:
                        transposes(n + 1, x1c[1 - p], xn_ok, hT_hi, xT_mm, (at.index(m),))
                    if m - 1 in ada:
                        spread_rows(ada[m - 1])
                    if m in ada:
                        multiply_piece(ada[m])
                    if m == max_at:
                        transpose_max(0)

            for n in range(2):
                multiply_piece(n)
                spread_rows(n)
            pe.wait_ge(ident_ok, 3)
            transposes(0, x1c[0], xn_ok, hT_hi, xT_mm)
            chunk(0, 0, at=T_AT_0, ada=ADA_AT[0])
            chunk(1, 1, ada=ADA_AT[1])
            with pe.Fori(0, 2) as i:
                for p in range(2):
                    chunk(i * 2 + LOOP + p, p)
            chunk(NCHUNK - 2, 0, max_after=FILLS_6)
            chunk(NCHUNK - 1, 1, nxt=False, max_after=FILLS_7, max_at=MAX_AT_7)
            assert next(fills, None) is None

            def max_scores(g, u, f):
                pe.wait_ge(a_max, g * FILLS + f - A_BANKS + 1)
                j = f % NQ
                nc.tensor.matmul(ps[:, (u + f) % A_BANKS, :], qs[u][0:M_ROW, f // NQ * P:(f // NQ + 1) * P],
                                 ks[u][0:M_ROW, j * CH:(j + 1) * CH], start=True, stop=True).then_inc(a_mm, 1)

            def scores(g, u, t, j):
                if t == 0 and j == 0:
                    pe.wait_ge(neg_in, g * 16 + 16)
                if not isinstance(g, int) or g or t or j >= B_BANKS:
                    pe.wait_ge(exp_ok, START + g * (NT * NQ) + t * NQ + j - B_BANKS + 1)
                nc.tensor.matmul(ps[:, A_BANKS + (u + t * NQ + j) % B_BANKS, :], ks[u][0:M_ROW + 1, t * P:(t + 1) * P],
                                 qs[u][0:M_ROW + 1, j * CH:(j + 1) * CH], start=True, stop=True).then_inc(b_mm, 1)

            def denominators(src, first, last):
                for j in range(NQ):
                    mm = nc.tensor.matmul(ps[j * DH:(j + 1) * DH, DEN_BANK, :], ones[:, 0:DH], src(j), start=first, stop=last)
                return mm

            def values(g, u, t):
                pe.wait_ge(exp_ok, START + g * (NT * NQ) + (t + 1) * NQ)
                if t == 0 and not (isinstance(g, int) and g == 0):
                    pe.wait_ge(o_raw, g)
                for j in range(NQ):
                    mm = nc.tensor.matmul(ps[j * DH:(j + 1) * DH, O_BANK, :], v_sb[u][:, t, :], prob[:, t % RING, j * CH:(j + 1) * CH],
                                          start=(t == 0), stop=(t == NT - 1))
                if t not in PE_TILES:
                    mm.then_inc(pv_mm, 1)

            def tile_sum(g, t):
                if t == PE_TILES[0] and not (isinstance(g, int) and g == 0):
                    pe.wait_ge(den_raw, g)
                denominators(lambda j: prob[:, t % RING, j * CH:(j + 1) * CH], t == PE_TILES[0], False).then_inc(pv_mm, 1)

            def finish_denominators(g):
                pe.wait_ge(add_ok, START + (g + 1) * (NADD * HALVES))
                denominators(lambda j: psum_acc[:, j * CH:(j + 1) * CH], False, True).then_inc(den_mm, 1)

            def last_values(g, u):
                values(g, u, NT - 1)
                if NT - 1 in PE_TILES:
                    tile_sum(g, NT - 1)

            def head(g, u, uses_next, prev, nxt, between={}):
                un = (u + 1) % NBUF
                if nxt:
                    pe.wait_ge(head_in[un], uses_next * (16 * LOADS))
                    pe.wait_ge(neg_ok, g + 1)
                fills = iter(range(FILLS if nxt else 0))

                def fill(t, place):
                    if nxt:
                        for _ in range(SPREAD[FILLS_AT[t]][place]):
                            max_scores(g + 1, un, next(fills))

                for t in range(NT):
                    scores(g, u, t, 0)
                    fill(t, 0)
                    scores(g, u, t, 1)
                    fill(t, 1)
                    if t == 0 and prev:
                        last_values(g - 1, (u + 2) % NBUF)
                    if t == 1 and prev:
                        finish_denominators(g - 1)
                    if t >= 2 and t - 2 in PE_TILES:
                        tile_sum(g, t - 2)
                    if t >= 1:
                        values(g, u, t - 1)
                    fill(t, 2)
                    if t in between:
                        between[t]()
                    scores(g, u, t, 2)
                    fill(t, 3)
                    scores(g, u, t, 3)
                    fill(t, 4)
                    if nxt and t == STEP_MAX:
                        transpose_max(g + 1)
                assert next(fills, None) is None
                if NT - 2 in PE_TILES:
                    tile_sum(g, NT - 2)

            pe.wait_ge(ones_row, 1)
            pe.wait_ge(v_ok, START + NCHUNK * TT)
            head(0, 0, 1, False, True)
            pe.wait_ge(ones_row, NBUF)
            nc.disable_value_cache = True
            with pe.Fori(0, G // NBUF) as i:
                for k in range(1, NBUF + 1):
                    head(i * NBUF + k, k % NBUF, i + 1 if k + 1 < NBUF else i + 2, True, True)
            nc.disable_value_cache = False
            def project_tile(n, t):
                if t < 2:
                    pe.wait_ge(h2_hi, START + n * KC)
                else:
                    pe.wait_ge(o_tmp, n * TT + t - 1)
                product(ps[:, t % 2, :], lambda s, kk: oT_r[:, s, kk, t * P:(t + 1) * P],
                        lambda s, kk: wo_r[:, s, kk, :]).then_inc(o_mm, 1)

            def project(n):
                pe.wait_ge(oT_lo, (n + 1) * KC)
                for t in range(TT):
                    project_tile(n, t)

            def transposes3(n, blocks):
                pe.wait_ge(o_tmp, (n + 1) * TT)
                transposes(n, xn3, xn3_ok, h2_hi, h2_mm, blocks)

            def first_projection(t):
                if t == 0:
                    pe.wait_ge(late_lo, len(late))
                    pe.wait_ge(w2_lo, 2)
                    pe.wait_ge(oT_lo, KC)
                project_tile(0, t)

            between = {STEP_PROJECT + t: lambda t=t: first_projection(t) for t in range(TT)}
            between[STEP_TRANSPOSE] = lambda: transposes3(0, (0, 1))
            head(G - 1, (G - 1) % NBUF, 0, True, False, between)
            last_values(G - 1, (G - 1) % NBUF)
            transposes3(0, (2, 3))
            finish_denominators(G - 1)

            def mlp1(n, f):
                if f >= 2:
                    pe.wait_ge(gelu_ok, START + n * FB + f - 1)
                else:
                    pe.wait_ge(gelu_ok, START + n * FB)
                product(ps[:, 2 + f % 2, :], lambda s, kk: w1_r[:, s, kk, f * P:(f + 1) * P],
                        lambda s, kk: h2T[:, s, kk, :]).then_inc(m1_mm, 1)

            def mlp2(n, f):
                pe.wait_ge(g_lo, START + n * FB + f + 1)
                if f == 0:
                    pe.wait_ge(y_ok, START + n * TT)
                    pe.wait_ge(o_raw, G)
                    pe.wait_ge(den_raw, G)
                for t in range(TT):
                    for s, r in ((0, 0), (0, 1), (1, 0)):
                        mm = nc.tensor.matmul(ps[:, 4 + t, :], g_r[:, f % 4, s, t * P:(t + 1) * P], w2_r[:, r, f, :],
                                              start=(f == 0 and s == r), stop=(f == FB - 1 and s == 1))
                mm.then_inc(m2_used, 1)

            def stage3(c, b, nxt):
                n = c * 2 + b
                pe.wait_ge(h2_lo, START + (n + 1) * KC)
                for f in range(AHEAD):
                    mlp1(n, f)
                for f in range(FB):
                    mlp2(n, f)
                    if f + AHEAD < FB:
                        mlp1(n, f + AHEAD)
                    if nxt and f == 0:
                        project(n + 1)
                    if nxt and f == FB - AHEAD - 1:
                        transposes3(n + 1, (0, 1))
                    if nxt and f == FB - AHEAD:
                        transposes3(n + 1, (2, 3))

            with pe.Fori(0, CPB - 1) as c:
                for b in range(2):
                    stage3(c, b, True)
            stage3(CPB - 1, 0, True)
            stage3(CPB - 1, 1, False)


def kernel(x, cond_1024, L0_cond_Wq, L0_cond_bq, L0_cond_Wk, L0_cond_bk, L0_cond_Wv, L0_cond_bv, L0_cond_Wo,
           L0_cond_bo, L0_cond_W1, L0_cond_b1, L0_cond_W2, L0_cond_b2, L0_cond_Wada, L0_cond_bada):
    import numpy as np
    import concourse.bacc as bacc
    from concourse.bass_utils import run_bass_kernel_spmd

    def columns(a):
        a = np.asarray(a)
        return np.ascontiguousarray(a.reshape(-1, P).T)

    c = np.asarray(cond_1024)
    inputs = {
        "x": np.asarray(x),
        "cT": np.ascontiguousarray(c.reshape(B, KC, P).transpose(2, 1, 0)),
        "wq": L0_cond_Wq, "wk": L0_cond_Wk, "wv": L0_cond_Wv, "wo": L0_cond_Wo, "w1": L0_cond_W1, "w2": L0_cond_W2,
        "wada": L0_cond_Wada, "bqT": columns(L0_cond_bq), "bkT": columns(L0_cond_bk), "b1T": columns(L0_cond_b1),
        "badaT": np.ascontiguousarray(columns(L0_cond_bada).reshape(P, 6, KC)), "bada": L0_cond_bada,
        "bv": L0_cond_bv, "bo": L0_cond_bo, "b2": L0_cond_b2,
    }
    nc = bacc.Bacc("TRN2", target_bir_lowering=False, num_devices=1)
    arrays, args = {}, []
    for name, a in inputs.items():
        a = np.ascontiguousarray(np.asarray(a))
        arrays[f"in_{name}"] = a
        args.append(nc.dram_tensor(f"in_{name}", a.shape, mybir.dt.from_np(a.dtype), kind="ExternalInput").ap())
    out = nc.dram_tensor("out_y", (B, L, D), F32, kind="ExternalOutput").ap()
    block_kernel(nc, *args, out)
    r = run_bass_kernel_spmd(nc, [arrays], core_ids=[0])
    return r.results[0]["out_y"]
```
